# Optimizing a Trainium2 kernel written in Bass

```python
import numpy as np
import jax
import jax.numpy as jnp

def _softmax(x, axis=-1):
    return jax.nn.softmax(x, axis=axis)

def _gelu(x):
    return jax.nn.gelu(x, approximate=True)

def _silu(x):
    return jax.nn.silu(x)

def _sigmoid(x):
    return jax.nn.sigmoid(x)

def _layernorm(x, axis=-1, eps=1e-05):
    m = jnp.mean(x, axis=axis, keepdims=True)
    v = jnp.var(x, axis=axis, keepdims=True)
    return (x - m) / jnp.sqrt(v + eps)

def _scatter_add(tgt, idx, src, axis=0):
    return tgt.at[idx].add(src)

def _segment_sum(src, seg, n):
    return jax.ops.segment_sum(src, seg, n)
kernel_name = 'mk_adj_preln_d1_adj_r2_cc79fe'

def setup_inputs(seed: int=0):
    np.random.seed(seed)
    _w = jnp.asarray

    def _rec_inputs():
        import jax
        import jax.numpy as jnp
        _gk = jax.random.key(seed)
        x = -0.0002928 + 1 * jax.random.normal(jax.random.fold_in(_gk, 1), (64, 128, 128), jnp.float32)
        _a = jax.random.bernoulli(jax.random.fold_in(_gk, 2), 0.0625, (64, 128, 128))
        adj = _a.astype(jnp.int32)
        return (x, adj)
    x, adj = _rec_inputs()

    def _L0_gnn_setup():
        import jax, jax.numpy as jnp
        import numpy as np
        OUT = 128
        NUM_LAYERS = 3

        def _gru_cell(inp, h, w_ih, w_hh, b_ih, b_hh):
            gi = inp @ w_ih.T + b_ih
            gh = h @ w_hh.T + b_hh
            i_r, i_z, i_n = jnp.split(gi, 3, axis=-1)
            h_r, h_z, h_n = jnp.split(gh, 3, axis=-1)
            r = jax.nn.sigmoid(i_r + h_r)
            z = jax.nn.sigmoid(i_z + h_z)
            n = jnp.tanh(i_n + r * h_n)
            return (1.0 - z) * n + z * h
        key = jax.random.key(seed)
        ks = jax.random.split(key, 8)
        B, N, D = (32, 256, 128)
        x = jax.random.normal(ks[0], (B, N, D), dtype=jnp.float32)
        adj = jax.random.randint(ks[1], (B, N, N), 0, 2, dtype=jnp.int32)
        s = 1.0 / np.sqrt(OUT)
        weight = jax.random.uniform(ks[2], (NUM_LAYERS, OUT, OUT), jnp.float32, -s, s)
        w_ih = jax.random.uniform(ks[3], (3 * OUT, OUT), jnp.float32, -s, s)
        w_hh = jax.random.uniform(ks[4], (3 * OUT, OUT), jnp.float32, -s, s)
        b_ih = jax.random.uniform(ks[5], (3 * OUT,), jnp.float32, -s, s)
        b_hh = jax.random.uniform(ks[6], (3 * OUT,), jnp.float32, -s, s)
        return {'x': x, 'adj': adj, 'weight': weight, 'w_ih': w_ih, 'w_hh': w_hh, 'b_ih': b_ih, 'b_hh': b_hh}
    _L0_gnn_all = _L0_gnn_setup()
    _L0_gnn_in = {k: v for k, v in _L0_gnn_all.items() if k in ('weight', 'w_ih', 'w_hh', 'b_ih', 'b_hh')}
    del _L0_gnn_all
    return {'x': x, 'adj': adj, 'L0_gnn_weight': _L0_gnn_in['weight'], 'L0_gnn_w_ih': _L0_gnn_in['w_ih'], 'L0_gnn_w_hh': _L0_gnn_in['w_hh'], 'L0_gnn_b_ih': _L0_gnn_in['b_ih'], 'L0_gnn_b_hh': _L0_gnn_in['b_hh']}

def reference(x, adj, L0_gnn_weight, L0_gnn_w_ih, L0_gnn_w_hh, L0_gnn_b_ih, L0_gnn_b_hh):
    import jax
    import jax.numpy as jnp

    def _L0_gnn_ref(x, adj, weight, w_ih, w_hh, b_ih, b_hh):
        import jax, jax.numpy as jnp
        import numpy as np
        OUT = 128
        NUM_LAYERS = 3

        def _gru_cell(inp, h, w_ih, w_hh, b_ih, b_hh):
            gi = inp @ w_ih.T + b_ih
            gh = h @ w_hh.T + b_hh
            i_r, i_z, i_n = jnp.split(gi, 3, axis=-1)
            h_r, h_z, h_n = jnp.split(gh, 3, axis=-1)
            r = jax.nn.sigmoid(i_r + h_r)
            z = jax.nn.sigmoid(i_z + h_z)
            n = jnp.tanh(i_n + r * h_n)
            return (1.0 - z) * n + z * h
        A = (adj != 0).astype(x.dtype)
        h = x
        L = weight.shape[0]
        for i in range(L):
            m = jnp.einsum('bnd,de->bne', h, weight[i])
            aggr = jnp.einsum('bst,bsd->btd', A, m)
            h = _gru_cell(aggr, h, w_ih, w_hh, b_ih, b_hh)
        return h
    h = jnp.maximum(_layernorm(x, axis=-1), 0.0)
    x = x + _L0_gnn_ref(h, adj, L0_gnn_weight, L0_gnn_w_ih, L0_gnn_w_hh, L0_gnn_b_ih, L0_gnn_b_hh)
    return x

_drawn_inputs = setup_inputs


def setup_inputs(seed=0):
    import zlib

    import numpy as np

    out = dict(_drawn_inputs(seed))
    spreads = {}
    factors = {}
    for name, (base, spread) in spreads.items():
        noise = np.random.default_rng([zlib.crc32(name.encode()), seed]).standard_normal(out[name].shape)
        drawn = base * np.exp(spread * noise) if base else spread * noise
        out[name] = jnp.asarray(drawn.astype(out[name].dtype))
    for name, factor in factors.items():
        out[name] = (out[name] * factor).astype(out[name].dtype)
    return out
```

```python
from contextlib import ExitStack

import concourse.bass as bass
from concourse import mybir


def gnn_residual_kernel(nc, x, adj, weight, w_ih, w_hh, b_ih, b_hh, out):
    f32, f32r, i32 = mybir.dt.float32, mybir.dt.float32r, mybir.dt.int32
    ALU = mybir.AluOpType
    ACT = mybir.ActivationFunctionType

    B, N, D = x.shape
    L = weight.shape[0]
    P = 128
    assert N == P and D == P and L == 3
    PER = 4
    COLS = PER * N
    GROUPS = B // PER
    EPS = 1e-5

    order = []
    for i in range(GROUPS + L - 1):
        order += [(l, i - l) for l in range(L) if 0 <= i - l < GROUPS]
    STEPS = len(order)
    at = {s: n for n, s in enumerate(order)}

    def transpose_slot(n):
        l, g = order[n]
        return max(n - 2, 0) if l == 0 else at[(l - 1, g)] + 2

    def aggregate_slot(n):
        return max(transpose_slot(n), n - 1)

    FIRST = 3 * L + 2
    PERIOD = 2 * L
    ROUNDS = (STEPS - 7 - FIRST) // PERIOD
    AFTER = FIRST + ROUNDS * PERIOD
    LAST = STEPS + 2

    x_v = x.rearrange("b n d -> n b d")
    adj_v = adj.rearrange("b s t -> s b t")
    out_v = out.rearrange("b n d -> n b d")

    ctx = ExitStack()
    with ctx:
        def sb(name, shape, dt=f32):
            return ctx.enter_context(nc.sbuf_tensor(name, shape, dt))

        def sem(name):
            return ctx.enter_context(nc.semaphore(name))

        def layer_sems(name):
            return [sem(f"{name}_{l}") for l in range(L)]

        x_all = sb("x_all", [P, B * D])
        mask_all = sb("mask_all", [P, B * N], f32r)
        adj_raw = [sb(f"adj_raw{p}", [P, PER, N], i32) for p in range(2)]
        out_rows = [sb(f"out_rows{p}", [P, PER, D]) for p in range(2)]
        ident = sb("ident", [P, P])
        w_nat = sb("w_nat", [P, L, P])
        wih_nat = sb("wih_nat", [P, 3, P])
        whh_nat = sb("whh_nat", [P, 3, P])
        wT = sb("wT", [P, L, P])
        wihT = sb("wihT", [P, 3 * P])
        v_hi = [sb(f"v_hi{l}", [P, 3 * P], f32r) for l in range(L)]
        v_lo = [sb(f"v_lo{l}", [P, 3 * P], f32r) for l in range(L)]
        whh_hi = sb("whh_hi", [P, 3 * P], f32r)
        whh_lo = sb("whh_lo", [P, 3 * P], f32r)
        bi = sb("bi", [P, 3])
        bh = sb("bh", [P, 3])
        b_rz = sb("b_rz", [P, 2])
        half_power = sb("half_power", [P, PER])
        stats = [sb(f"stats{p}", [P, PER, 6]) for p in range(2)]
        mean_var = [sb(f"mean_var{p}", [P, PER, 2]) for p in range(2)]
        var_eps = [sb(f"var_eps{p}", [P, PER]) for p in range(2)]
        rstd = [sb(f"rstd{p}", [P, PER]) for p in range(2)]
        normed = sb("normed", [P, COLS])
        relu_nat = [sb(f"relu_nat{p}", [P, COLS]) for p in range(2)]
        nat_hi = [sb(f"nat_hi{l}", [P, COLS], f32r) for l in range(L)]
        nat_lo = [sb(f"nat_lo{l}", [P, COLS], f32r) for l in range(L)]
        g_hi = [sb(f"g_hi{l}", [P, COLS], f32r) for l in range(L)]
        g_lo = [sb(f"g_lo{l}", [P, COLS], f32r) for l in range(L)]
        h = [[sb(f"h{l}_{p}", [P, COLS]) for p in range(2)] for l in range(L + 1)]
        h_hi = [[sb(f"h_hi{l}_{p}", [P, COLS], f32r) for p in range(2)] for l in range(L)]
        h_lo = [[sb(f"h_lo{l}_{p}", [P, COLS], f32r) for p in range(2)] for l in range(L)]
        r_sb = [sb(f"r{l}", [P, COLS]) for l in range(L)]
        z_sb = [sb(f"z{l}", [P, COLS]) for l in range(L)]
        rh = [sb(f"rh{l}", [P, COLS]) for l in range(L)]
        n_sb = [sb(f"n{l}", [P, COLS]) for l in range(L)]
        zd = [sb(f"zd{l}", [P, COLS]) for l in range(L)]

        def bank(name):
            return ctx.enter_context(nc.psum_tensor(name, [P, COLS], f32))

        ps_t, ps_out, ps_g, ps_hn = bank("ps_t"), bank("ps_out"), bank("ps_g"), bank("ps_hn")
        ps_r, ps_in, ps_z, ps_w = bank("ps_r"), bank("ps_in"), bank("ps_z"), bank("ps_w")
        ps_whhT, ps_wihT, ps_wT, ps_v = ps_hn, ps_r, ps_in, [ps_z, ps_w, ps_out]

        x_loaded = [sem(f"x_loaded{p}") for p in range(2)]
        adj_loaded = [sem(f"adj_loaded{p}") for p in range(2)]
        stored = [sem(f"stored{p}") for p in range(2)]
        w_loaded, wih_loaded, whh_loaded, b_loaded = sem("w_loaded"), sem("wih_loaded"), sem("whh_loaded"), sem("b_loaded")
        ident_zero, ident_ready, power_ready = sem("ident_zero"), sem("ident_ready"), sem("power_ready")
        wT_made, wihT_made, whhT_made, v_made = sem("wT_made"), sem("wihT_made"), sem("whhT_made"), sem("v_made")
        wT_ready, wihT_ready, bias_ready = sem("wT_ready"), sem("wihT_ready"), sem("bias_ready")
        weights_hi, weights_lo = sem("weights_hi"), sem("weights_lo")
        bn_done, stats_done, var_done, rstd_done = sem("bn_done"), sem("stats_done"), sem("var_done"), sem("rstd_done")
        normed_done, relu_done, mask_done, h0_done = sem("normed_done"), sem("relu_done"), sem("mask_done"), sem("h0_done")
        transposed = layer_sems("transposed")
        nat_hi_done, nat_lo_done = layer_sems("nat_hi_done"), layer_sems("nat_lo_done")
        h_hi_done, h_lo_done = layer_sems("h_hi_done"), layer_sems("h_lo_done")
        aggregated = layer_sems("aggregated")
        g_hi_done, g_lo_done = layer_sems("g_hi_done"), layer_sems("g_lo_done")
        hn_made, r_made, in_made, z_made = (layer_sems(s) for s in ("hn_made", "r_made", "in_made", "z_made"))
        r_done, z_done, rh_done, pre_done = (layer_sems(s) for s in ("r_done", "z_done", "rh_done", "pre_done"))
        n_done, diff_done, zd_done, h_done = (layer_sems(s) for s in ("n_done", "diff_done", "zd_done", "h_done"))
        out_transposed, out_ready = sem("out_transposed"), sem("out_ready")

        class Step:
            def __init__(self, n, it):
                self.n, self.l, self.g0 = n, *order[n]
                self.it = it
                self.g = self.g0 + 2 * it
                self.parity = self.g0 % 2
                self.pair = self.g0 // 2 + it
                self.in_loop = not isinstance(it, int)

            def before(self):
                return Step(self.n - 1, self.it) if self.n else None

        def steps_in(slot_of, s, it):
            return [Step(n, it) for n in range(max(s - 3, 0), min(s + 6, STEPS)) if slot_of(n) == s]

        transpose_order = sorted(range(STEPS), key=lambda n: (transpose_slot(n), n))

        def transposed_before(st):
            i = transpose_order.index(st.n)
            return Step(transpose_order[i - 1], st.it) if i else None

        def first_steps(s, it, lead, done):
            n = s + lead
            return [Step(n, it)] if n < STEPS and order[n][0] == 0 and order[n][1] >= done else []

        def run_slots(eng, slot):
            for s in range(FIRST):
                slot(s, 0)
            with eng.Fori(0, ROUNDS) as it:
                for s in range(FIRST, FIRST + PERIOD):
                    slot(s, it)
            for s in range(AFTER, LAST):
                slot(s, 0)

        def gates(s, it):
            return [Step(s, it)] if 0 <= s < STEPS else []

        EARLY = [Step(at[(0, g)], 0) for g in range(3)]

        block = ctx.enter_context(nc.Block())

        @block.sync
        def _(sp):
            def load(g, p):
                sp.dma_start(x_all[:, bass.ts(g, COLS)].rearrange("n (b d) -> n b d", d=D),
                             x_v[:, bass.ts(g, PER), :]).then_inc(x_loaded[p], 16)
                sp.dma_start(adj_raw[p][:, :, :], adj_v[:, bass.ts(g, PER), :]).then_inc(adj_loaded[p], 16)

            def load_after(g, p):
                sp.wait_ge(stats_done, g + 1)
                sp.wait_ge(mask_done, g + 1)
                load(g + 2, p)

            def store(g, p):
                sp.wait_ge(out_ready, g + 1)
                sp.dma_start(out_v[:, bass.ts(g, PER), :], out_rows[p][:, :, :]).then_inc(stored[p], 16)

            STORES_BEHIND = 4
            for p in range(2):
                load(p, p)
            for g in range(STORES_BEHIND):
                load_after(g, g % 2)
            with sp.Fori(0, (GROUPS - 2 - STORES_BEHIND) // 2) as it:
                for p in range(2):
                    load_after(2 * it + (STORES_BEHIND + p), p)
                    store(2 * it + p, p)
            for g in range(GROUPS - 2 - STORES_BEHIND, GROUPS):
                store(g, g % 2)
            for p in range(2):
                sp.wait_ge(stored[p], 16 * (GROUPS // 2))

        @block.gpsimd
        def _(pool):
            pool.memset(ident[:, :], 0.0).then_inc(ident_zero, 1)
            pool.memset(half_power[:, :], -0.5).then_inc(power_ready, 1)
            pool.wait_ge(ident_zero, 1)
            pool.affine_select(out=ident[:, :], in_=ident[:, :], compare_op=ALU.not_equal, fill=1.0, base=0,
                               pattern=[[-1, P]], channel_multiplier=1).then_inc(ident_ready, 1)
            pool.wait_ge(power_ready, 1)

            def inverse_deviation(st):
                pool.wait_ge(var_done, st.g + 1)
                pool.tensor_tensor(rstd[st.parity][:, :], var_eps[st.parity][:, :], half_power[:, :], ALU.pow) \
                    .then_inc(rstd_done, 1)

            def first_nat_lo(st):
                pool.wait_ge(nat_hi_done[0], st.g + 1)
                if st.g0 or st.in_loop:
                    pool.wait_ge(aggregated[0], st.g)
                pool.tensor_tensor(nat_lo[0][:, :], relu_nat[st.parity][:, :], nat_hi[0][:, :].bitcast(f32),
                                   ALU.subtract).then_inc(nat_lo_done[0], 1)

            def difference(st):
                pool.wait_ge(n_done[st.l], st.g + 1)
                if st.l == 0:
                    pool.wait_ge(h0_done, st.g + 1)
                if st.g0 or st.in_loop:
                    pool.wait_ge(h_done[st.l], st.g)
                pool.tensor_tensor(zd[st.l][:, :], h[st.l][st.parity][:, :], n_sb[st.l][:, :], ALU.subtract) \
                    .then_inc(diff_done[st.l], 1)

            def update(st):
                pool.wait_ge(z_done[st.l], st.g + 1)
                pool.wait_ge(diff_done[st.l], st.g + 1)
                pool.tensor_tensor(zd[st.l][:, :], z_sb[st.l][:, :], zd[st.l][:, :], ALU.mult) \
                    .then_inc(zd_done[st.l], 1)

            def state_lo(st):
                pool.wait_ge(h_hi_done[st.l + 1], st.g + 1)
                pool.tensor_tensor(h_lo[st.l + 1][st.parity][:, :], h[st.l + 1][st.parity][:, :],
                                   h_hi[st.l + 1][st.parity][:, :].bitcast(f32), ALU.subtract) \
                    .then_inc(h_lo_done[st.l + 1], 1)

            def slot(s, it):
                if s == 0:
                    for st in EARLY[:2]:
                        inverse_deviation(st)
                        first_nat_lo(st)
                    inverse_deviation(EARLY[2])
                for st in gates(s - 1, it):
                    difference(st)
                    update(st)
                for st in gates(s - 2, it):
                    if st.l < L - 1:
                        state_lo(st)
                for st in first_steps(s, it, 4, 3):
                    inverse_deviation(st)
                for st in first_steps(s, it, 3, 2):
                    first_nat_lo(st)

            run_slots(pool, slot)

        @block.scalar
        def _(act):
            act.dma_start(w_nat[:, :, :], weight.rearrange("l d e -> d l e")).then_inc(w_loaded, 16)
            act.dma_start(wih_nat[:, :, :], w_ih.rearrange("(c p) e -> p c e", p=P)).then_inc(wih_loaded, 16)
            act.dma_start(whh_nat[:, :, :], w_hh.rearrange("(c p) e -> p c e", p=P)).then_inc(whh_loaded, 16)
            with nc.allow_non_contiguous_dma(reason="two columns of biases"):
                act.dma_start(bi[:, :], b_ih.rearrange("(c p) -> p c", p=P)).then_inc(b_loaded, 16)
                act.dma_start(bh[:, :], b_hh.rearrange("(c p) -> p c", p=P)).then_inc(b_loaded, 16)
            act.wait_ge(wT_made, 1)
            act.copy(wT[:, :, :].rearrange("p l d -> p (l d)"), ps_wT[:, 0:L * P]).then_inc(wT_ready, 1)
            act.wait_ge(whhT_made, 1)
            act.copy(whh_hi[:, :], ps_whhT[:, 0:3 * P]).then_inc(weights_hi, 1)
            for l in range(L):
                act.wait_ge(v_made, l + 1)
                act.copy(v_hi[l][:, :], ps_v[l][:, 0:3 * P]).then_inc(weights_hi, 1)

            def first_nat_hi(st):
                act.wait_ge(relu_done, st.g + 1)
                if st.g0 or st.in_loop:
                    act.wait_ge(aggregated[0], st.g)
                act.copy(nat_hi[0][:, :], relu_nat[st.parity][:, :]).then_inc(nat_hi_done[0], 1)

            def transposed_hi(st):
                act.wait_ge(transposed[st.l], st.g + 1)
                if st.l == 0:
                    if st.g0 >= 2 or st.in_loop:
                        act.wait_ge(z_made[0], st.g - 1)
                        act.wait_ge(diff_done[0], st.g - 1)
                    act.copy(h_hi[0][st.parity][:, :], ps_t[:, :]).then_inc(h_hi_done[0], 1)
                    act.copy(h[0][st.parity][:, :], ps_t[:, :]).then_inc(h0_done, 1)
                else:
                    if st.g0 or st.in_loop:
                        act.wait_ge(aggregated[st.l], st.g)
                    act.copy(nat_hi[st.l][:, :], ps_t[:, :]).then_inc(nat_hi_done[st.l], 1)

            def aggregate_hi(st):
                act.wait_ge(aggregated[st.l], st.g + 1)
                if st.g0 or st.in_loop:
                    act.wait_ge(z_made[st.l], st.g)
                act.copy(g_hi[st.l][:, :], ps_g[:, :]).then_inc(g_hi_done[st.l], 1)

            def reset_gate(st):
                act.wait_ge(r_made[st.l], st.g + 1)
                if st.g0 or st.in_loop:
                    act.wait_ge(rh_done[st.l], st.g)
                act.activation(r_sb[st.l][:, :], ps_r[:, :], ACT.Sigmoid, bias=b_rz[:, 0:1]).then_inc(r_done[st.l], 1)

            def update_gate(st):
                act.wait_ge(z_made[st.l], st.g + 1)
                if st.g0 or st.in_loop:
                    act.wait_ge(zd_done[st.l], st.g)
                act.activation(z_sb[st.l][:, :], ps_z[:, :], ACT.Sigmoid, bias=b_rz[:, 1:2]).then_inc(z_done[st.l], 1)

            def candidate(st):
                act.wait_ge(pre_done[st.l], st.g + 1)
                if st.g0 or st.in_loop:
                    act.wait_ge(h_done[st.l], st.g)
                act.activation(n_sb[st.l][:, :], rh[st.l][:, :], ACT.Tanh, bias=bi[:, 2:3]).then_inc(n_done[st.l], 1)

            def state_hi(st):
                act.wait_ge(h_done[st.l], st.g + 1)
                if st.g0 >= 2 or st.in_loop:
                    act.wait_ge(z_made[st.l + 1], st.g - 1)
                act.copy(h_hi[st.l + 1][st.parity][:, :], h[st.l + 1][st.parity][:, :]).then_inc(h_hi_done[st.l + 1], 1)

            def slot(s, it):
                if s == 0:
                    for st in EARLY[:2]:
                        first_nat_hi(st)
                    act.wait_ge(bias_ready, 1)
                for st in gates(s - 1, it):
                    update_gate(st)
                for st in steps_in(transpose_slot, s, it):
                    transposed_hi(st)
                own = [st for st in steps_in(aggregate_slot, s, it) if st.n == s]
                for st in own:
                    aggregate_hi(st)
                for st in gates(s, it):
                    reset_gate(st)
                for st in gates(s - 1, it):
                    if st.l < L - 1:
                        state_hi(st)
                for st in steps_in(aggregate_slot, s, it):
                    if st.n > s:
                        aggregate_hi(st)
                for st in gates(s, it):
                    candidate(st)
                for st in first_steps(s, it, 3, 2):
                    first_nat_hi(st)

            run_slots(act, slot)

        @block.vector
        def _(dve):
            def mask_and_statistics(st):
                dve.wait_ge(x_loaded[st.parity], 16 * (st.pair + 1))
                for b in range(PER):
                    ins = dve.bn_stats(stats[st.parity][:, b, :], x_all[:, bass.ds(st.g * COLS + b * D, D)])
                ins.then_inc(bn_done, 1)
                dve.wait_ge(adj_loaded[st.parity], 16 * (st.pair + 1))
                dve.wait_ge(bn_done, st.g + 1)
                dve.tensor_scalar(mask_all[:, bass.ts(st.g, COLS)],
                                  adj_raw[st.parity][:, :, :].rearrange("s b t -> s (b t)"),
                                  0, None, ALU.not_equal).then_inc(mask_done, 1)
                for b in range(PER):
                    ins = dve.bn_aggr(mean_var[st.parity][:, b, :], stats[st.parity][:, b, :])
                ins.then_inc(stats_done, 1)
                dve.wait_ge(stats_done, st.g + 1)
                dve.tensor_scalar(var_eps[st.parity][:, :], mean_var[st.parity][:, :, 1], EPS, None, ALU.add) \
                    .then_inc(var_done, 1)

            def normalise(st):
                dve.wait_ge(rstd_done, st.g + 1)
                for b in range(PER):
                    ins = dve.tensor_scalar(normed[:, b * D:(b + 1) * D], x_all[:, bass.ds(st.g * COLS + b * D, D)],
                                            mean_var[st.parity][:, b, 0:1], rstd[st.parity][:, b:b + 1],
                                            ALU.subtract, ALU.mult)
                ins.then_inc(normed_done, 1)
                dve.wait_ge(normed_done, st.g + 1)
                if st.g0 >= 2 or st.in_loop:
                    dve.wait_ge(nat_lo_done[0], st.g - 1)
                    dve.wait_ge(transposed[0], st.g - 1)
                dve.tensor_scalar(relu_nat[st.parity][:, :], normed[:, :], 0.0, None, ALU.max).then_inc(relu_done, 1)

            def transposed_lo(st):
                if st.l == 0:
                    dve.wait_ge(h0_done, st.g + 1)
                    dve.tensor_tensor(h_lo[0][st.parity][:, :], ps_t[:, :], h_hi[0][st.parity][:, :].bitcast(f32),
                                      ALU.subtract).then_inc(h_lo_done[0], 1)
                else:
                    dve.wait_ge(nat_hi_done[st.l], st.g + 1)
                    dve.tensor_tensor(nat_lo[st.l][:, :], ps_t[:, :], nat_hi[st.l][:, :].bitcast(f32),
                                      ALU.subtract).then_inc(nat_lo_done[st.l], 1)

            def aggregate_lo(st):
                dve.wait_ge(g_hi_done[st.l], st.g + 1)
                dve.tensor_tensor(g_lo[st.l][:, :], ps_g[:, :], g_hi[st.l][:, :].bitcast(f32), ALU.subtract) \
                    .then_inc(g_lo_done[st.l], 1)

            def reset_product(st):
                dve.wait_ge(hn_made[st.l], st.g + 1)
                dve.wait_ge(r_done[st.l], st.g + 1)
                if st.g0 or st.in_loop:
                    dve.wait_ge(n_done[st.l], st.g)
                dve.scalar_tensor_tensor(out=rh[st.l][:, :], in0=ps_hn[:, :], scalar=bh[:, 2:3], in1=r_sb[st.l][:, :],
                                         op0=ALU.add, op1=ALU.mult).then_inc(rh_done[st.l], 1)

            def candidate_input(st):
                dve.wait_ge(in_made[st.l], st.g + 1)
                dve.wait_ge(rh_done[st.l], st.g + 1)
                dve.tensor_tensor(rh[st.l][:, :], ps_in[:, :], rh[st.l][:, :], ALU.add).then_inc(pre_done[st.l], 1)

            def new_state(st):
                dve.wait_ge(zd_done[st.l], st.g + 1)
                dve.tensor_tensor(h[st.l + 1][st.parity][:, :], n_sb[st.l][:, :], zd[st.l][:, :], ALU.add) \
                    .then_inc(h_done[st.l], 1)

            def residual(st):
                dve.wait_ge(out_transposed, st.g + 1)
                if st.g0 >= 2 or st.in_loop:
                    dve.wait_ge(stored[st.parity], 16 * st.pair)
                dve.tensor_tensor(out_rows[st.parity][:, :, :].rearrange("n b d -> n (b d)"), ps_out[:, :],
                                  x_all[:, bass.ts(st.g, COLS)], ALU.add).then_inc(out_ready, 1)

            mask_and_statistics(EARLY[0])
            normalise(EARLY[0])

            dve.wait_ge(wihT_made, 1)
            dve.tensor_copy(wihT[:, :], ps_wihT[:, 0:3 * P]).then_inc(wihT_ready, 1)
            dve.wait_ge(weights_hi, 1)
            dve.tensor_tensor(whh_lo[:, :], ps_whhT[:, 0:3 * P], whh_hi[:, :].bitcast(f32), ALU.subtract) \
                .then_inc(weights_lo, 1)
            dve.wait_ge(b_loaded, 32)
            dve.tensor_tensor(b_rz[:, :], bi[:, 0:2], bh[:, 0:2], ALU.add).then_inc(bias_ready, 1)
            for l in range(L):
                dve.wait_ge(weights_hi, l + 2)
                dve.tensor_tensor(v_lo[l][:, :], ps_v[l][:, 0:3 * P], v_hi[l][:, :].bitcast(f32), ALU.subtract) \
                    .then_inc(weights_lo, 1)

            def slot(s, it):
                if s == 0:
                    for st in EARLY[1:]:
                        mask_and_statistics(st)
                        normalise(st)
                for st in steps_in(transpose_slot, s, it):
                    transposed_lo(st)
                for st in steps_in(aggregate_slot, s, it):
                    if st.n == s:
                        aggregate_lo(st)
                for st in first_steps(s, it, 4, 3):
                    mask_and_statistics(st)
                for st in first_steps(s, it, 3, 3):
                    normalise(st)
                for st in gates(s - 1, it):
                    new_state(st)
                for st in gates(s, it):
                    reset_product(st)
                    candidate_input(st)
                for st in steps_in(aggregate_slot, s, it):
                    if st.n > s:
                        aggregate_lo(st)
                for st in gates(s - 2, it):
                    if st.l == L - 1:
                        residual(st)

            run_slots(dve, slot)

        @block.tensor
        def _(pe):
            def transpose4(dst, src):
                for b in range(PER):
                    ins = pe.transpose(dst[:, b * P:(b + 1) * P], src[:, b * P:(b + 1) * P], ident[:, :])
                return ins

            def transpose_state(st):
                if st.l == 0:
                    src = relu_nat[st.parity]
                    pe.wait_ge(relu_done, st.g + 1)
                else:
                    src = h[st.l][st.parity]
                    pe.wait_ge(h_done[st.l - 1], st.g + 1)
                last = transposed_before(st)
                if last and last.l == 0:
                    pe.wait_ge(h_lo_done[0], last.g + 1)
                elif last:
                    pe.wait_ge(nat_lo_done[last.l], last.g + 1)
                transpose4(ps_t, src).then_inc(transposed[st.l], 1)

            def transpose_out(st):
                pe.wait_ge(h_done[L - 1], st.g + 1)
                if st.g0 or st.in_loop:
                    pe.wait_ge(out_ready, st.g)
                transpose4(ps_out, h[L][st.parity]).then_inc(out_transposed, 1)

            def aggregate(st):
                pe.wait_ge(nat_hi_done[st.l], st.g + 1)
                pe.wait_ge(nat_lo_done[st.l], st.g + 1)
                if st.l == 0:
                    pe.wait_ge(mask_done, st.g + 1)
                last = st.before()
                if last:
                    pe.wait_ge(g_lo_done[last.l], last.g + 1)
                for b in range(PER):
                    cols = slice(b * P, (b + 1) * P)
                    mask = mask_all[:, bass.ds(st.g * COLS + b * N, N)]
                    pe.matmul(ps_g[:, cols], nat_hi[st.l][:, cols], mask, start=True, stop=False)
                    ins = pe.matmul(ps_g[:, cols], nat_lo[st.l][:, cols], mask, start=False, stop=True)
                ins.then_inc(aggregated[st.l], 1)

            def product(ps, w_hi, w_lo, gate, a_hi, a_lo, start, stop):
                cols = slice(gate * P, (gate + 1) * P)
                pe.matmul(ps[:, :], w_hi[:, cols], a_hi[:, :], start=start, stop=False)
                pe.matmul(ps[:, :], w_hi[:, cols], a_lo[:, :], start=False, stop=False)
                return pe.matmul(ps[:, :], w_lo[:, cols], a_hi[:, :], start=False, stop=stop)

            def state_part(st, ps, gate, stop):
                return product(ps, whh_hi, whh_lo, gate, h_hi[st.l][st.parity], h_lo[st.l][st.parity], True, stop)

            def aggregate_part(st, ps, gate, start):
                return product(ps, v_hi[st.l], v_lo[st.l], gate, g_hi[st.l], g_lo[st.l], start, True)

            def hidden_candidate(st):
                pe.wait_ge(h_hi_done[st.l], st.g + 1)
                pe.wait_ge(h_lo_done[st.l], st.g + 1)
                last = st.before()
                if last:
                    pe.wait_ge(rh_done[last.l], last.g + 1)
                state_part(st, ps_hn, 2, True).then_inc(hn_made[st.l], 1)

            def reset(st):
                last = st.before()
                if last:
                    pe.wait_ge(r_done[last.l], last.g + 1)
                state_part(st, ps_r, 0, False)
                pe.wait_ge(g_hi_done[st.l], st.g + 1)
                pe.wait_ge(g_lo_done[st.l], st.g + 1)
                aggregate_part(st, ps_r, 0, False).then_inc(r_made[st.l], 1)

            def input_candidate(st):
                last = st.before()
                if last:
                    pe.wait_ge(pre_done[last.l], last.g + 1)
                aggregate_part(st, ps_in, 2, True).then_inc(in_made[st.l], 1)

            def update(st):
                last = st.before()
                if last:
                    pe.wait_ge(z_done[last.l], last.g + 1)
                state_part(st, ps_z, 1, False)
                aggregate_part(st, ps_z, 1, False).then_inc(z_made[st.l], 1)

            pe.wait_ge(ident_ready, 1)
            pe.wait_ge(w_loaded, 16)
            for l in range(L):
                ins = pe.transpose(ps_wT[:, l * P:(l + 1) * P], w_nat[:, l, :], ident[:, :])
            ins.then_inc(wT_made, 1)
            pe.wait_ge(wih_loaded, 16)
            for c in range(3):
                ins = pe.transpose(ps_wihT[:, c * P:(c + 1) * P], wih_nat[:, c, :], ident[:, :])
            ins.then_inc(wihT_made, 1)
            pe.wait_ge(whh_loaded, 16)
            for c in range(3):
                ins = pe.transpose(ps_whhT[:, c * P:(c + 1) * P], whh_nat[:, c, :], ident[:, :])
            ins.then_inc(whhT_made, 1)
            pe.wait_ge(wT_ready, 1)
            pe.wait_ge(wihT_ready, 1)
            for l in range(L):
                pe.matmul(ps_v[l][:, 0:3 * P], wT[:, l, :], wihT[:, :], start=True, stop=True).then_inc(v_made, 1)

            def slot(s, it):
                if s == 0:
                    transpose_state(EARLY[0])
                    aggregate(EARLY[0])
                    pe.wait_ge(weights_lo, L + 1)
                for st in steps_in(transpose_slot, s, it):
                    if st.n:
                        transpose_state(st)
                for st in gates(s - 2, it):
                    if st.l == L - 1:
                        transpose_out(st)
                for st in steps_in(aggregate_slot, s, it):
                    if st.n == s and st.n:
                        aggregate(st)
                for st in gates(s, it):
                    hidden_candidate(st)
                    reset(st)
                for st in steps_in(aggregate_slot, s, it):
                    if st.n > s:
                        aggregate(st)
                for st in gates(s, it):
                    input_candidate(st)
                    update(st)

            run_slots(pe, slot)


_INS = ["x", "adj", "L0_gnn_weight", "L0_gnn_w_ih", "L0_gnn_w_hh", "L0_gnn_b_ih", "L0_gnn_b_hh"]
_OUTS = [((64, 128, 128), "float32")]


def kernel(**inputs):
    import numpy as _np
    import concourse.bacc as _bacc
    from concourse import mybir as _mybir
    from concourse.bass_utils import run_bass_kernel_spmd as _run

    nc = _bacc.Bacc("TRN2", target_bir_lowering=False, num_devices=1)
    arrays, args = {}, []
    for name in _INS:
        a = _np.ascontiguousarray(inputs[name])
        arrays[f"in_{name}_dram"] = a
        args.append(nc.dram_tensor(f"in_{name}_dram", a.shape, _mybir.dt.from_np(a.dtype), kind="ExternalInput").ap())
    for i, (shape, dtype) in enumerate(_OUTS):
        dt = _mybir.dt.from_np(_np.dtype(dtype))
        args.append(nc.dram_tensor(f"out_{i}_dram", shape, dt, kind="ExternalOutput").ap())
    gnn_residual_kernel(nc, *args)
    r = _run(nc, [arrays], core_ids=[0])
    return r.results[0]["out_0_dram"]
```

```python
from contextlib import ExitStack

import concourse.bass as bass
from concourse import mybir


def gnn_residual_kernel(nc, x, adj, weight, w_ih, w_hh, b_ih, b_hh, out):
    f32, f32r, i32 = mybir.dt.float32, mybir.dt.float32r, mybir.dt.int32
    ALU = mybir.AluOpType
    ACT = mybir.ActivationFunctionType

    B, N, D = x.shape
    L = weight.shape[0]
    P = 128
    assert N == P and D == P and L == 3
    PER = 4
    COLS = PER * N
    GROUPS = B // PER
    EPS = 1e-5

    order = []
    for i in range(GROUPS + L - 1):
        order += [(l, i - l) for l in range(L) if 0 <= i - l < GROUPS]
    STEPS = len(order)
    at = {s: n for n, s in enumerate(order)}

    def transpose_slot(n):
        l, g = order[n]
        return max(n - 2, 0) if l == 0 else at[(l - 1, g)] + 2

    def aggregate_slot(n):
        return max(transpose_slot(n) if order[n][0] else 0, n - 1)

    FIRST = 3 * L + 2
    PERIOD = 2 * L
    ROUNDS = (STEPS - 7 - FIRST) // PERIOD
    AFTER = FIRST + ROUNDS * PERIOD
    LAST = STEPS + 2

    x_v = x.rearrange("b n d -> n b d")
    adj_v = adj.rearrange("b s t -> s b t")
    out_v = out.rearrange("b n d -> n b d")

    ctx = ExitStack()
    with ctx:
        def sb(name, shape, dt=f32):
            return ctx.enter_context(nc.sbuf_tensor(name, shape, dt))

        def sem(name):
            return ctx.enter_context(nc.semaphore(name))

        def layer_sems(name):
            return [sem(f"{name}_{l}") for l in range(L)]

        x_all = sb("x_all", [P, B * D])
        mask_all = sb("mask_all", [P, B * N])
        adj_raw = [sb(f"adj_raw{p}", [P, PER, N], i32) for p in range(2)]
        out_rows = [sb(f"out_rows{p}", [P, PER, D]) for p in range(2)]
        ident = sb("ident", [P, P])
        w_nat = sb("w_nat", [P, L, P])
        wih_nat = sb("wih_nat", [P, 3, P])
        whh_nat = sb("whh_nat", [P, 3, P])
        wT = sb("wT", [P, L, P])
        wihT = sb("wihT", [P, 3 * P])
        v_hi = [sb(f"v_hi{l}", [P, 3 * P], f32r) for l in range(L)]
        v_lo = [sb(f"v_lo{l}", [P, 3 * P], f32r) for l in range(L)]
        whh_hi = sb("whh_hi", [P, 3 * P], f32r)
        whh_lo = sb("whh_lo", [P, 3 * P], f32r)
        bi = sb("bi", [P, 3])
        bh = sb("bh", [P, 3])
        b_rz = sb("b_rz", [P, 2])
        half_power = sb("half_power", [P, PER])
        warm = sb("warm", [P, PER])
        stats = [sb(f"stats{p}", [P, PER, 6]) for p in range(2)]
        mean_var = [sb(f"mean_var{p}", [P, PER, 2]) for p in range(2)]
        var_eps = [sb(f"var_eps{p}", [P, PER]) for p in range(2)]
        rstd = [sb(f"rstd{p}", [P, PER]) for p in range(2)]
        relu_nat = [sb(f"relu_nat{p}", [P, COLS]) for p in range(2)]
        nat = [None] + [sb(f"nat{l}", [P, COLS]) for l in range(1, L)]
        g_hi = [sb(f"g_hi{l}", [P, COLS], f32r) for l in range(L)]
        g_lo = [sb(f"g_lo{l}", [P, COLS], f32r) for l in range(L)]
        h = [[sb(f"h{l}_{p}", [P, COLS]) for p in range(2)] for l in range(L + 1)]
        h_hi = [[sb(f"h_hi{l}_{p}", [P, COLS], f32r) for p in range(2)] for l in range(L)]
        h_lo = [[sb(f"h_lo{l}_{p}", [P, COLS], f32r) for p in range(2)] for l in range(L)]
        r_sb = [sb(f"r{l}", [P, COLS]) for l in range(L)]
        z_sb = [sb(f"z{l}", [P, COLS]) for l in range(L)]
        rh = [sb(f"rh{l}", [P, COLS]) for l in range(L)]
        n_sb = [sb(f"n{l}", [P, COLS]) for l in range(L)]
        zd = [sb(f"zd{l}", [P, COLS]) for l in range(L)]

        def bank(name):
            return ctx.enter_context(nc.psum_tensor(name, [P, COLS], f32))

        ps_t, ps_out, ps_g, ps_hn = bank("ps_t"), bank("ps_out"), bank("ps_g"), bank("ps_hn")
        ps_r, ps_in, ps_z, ps_w = bank("ps_r"), bank("ps_in"), bank("ps_z"), bank("ps_w")
        ps_whhT, ps_wihT, ps_wT, ps_v = ps_hn, ps_r, ps_in, [ps_w, ps_out, ps_w]

        x_loaded = [sem(f"x_loaded{p}") for p in range(2)]
        adj_loaded = [sem(f"adj_loaded{p}") for p in range(2)]
        stored = [sem(f"stored{p}") for p in range(2)]
        w_loaded, wih_loaded, whh_loaded, b_loaded = sem("w_loaded"), sem("wih_loaded"), sem("whh_loaded"), sem("b_loaded")
        ident_zero, ident_ready, power_ready = sem("ident_zero"), sem("ident_ready"), sem("power_ready")
        wT_made, wihT_made, whhT_made, v_made = sem("wT_made"), sem("wihT_made"), sem("whhT_made"), sem("v_made")
        wT_ready, wihT_ready, bias_ready = sem("wT_ready"), sem("wihT_ready"), sem("bias_ready")
        weights_hi, weights_lo = sem("weights_hi"), sem("weights_lo")
        bn_done, stats_done, var_done, rstd_done = sem("bn_done"), sem("stats_done"), sem("var_done"), sem("rstd_done")
        normed_done, relu_done, mask_done, h0_done = sem("normed_done"), sem("relu_done"), sem("mask_done"), sem("h0_done")
        transposed = layer_sems("transposed")
        nat_done = layer_sems("nat_done")
        h_hi_done, h_lo_done = layer_sems("h_hi_done"), layer_sems("h_lo_done")
        aggregated = layer_sems("aggregated")
        g_hi_done, g_lo_done = layer_sems("g_hi_done"), layer_sems("g_lo_done")
        hn_made, r_made, in_made, z_made = (layer_sems(s) for s in ("hn_made", "r_made", "in_made", "z_made"))
        r_done, z_done, rh_done, pre_done = (layer_sems(s) for s in ("r_done", "z_done", "rh_done", "pre_done"))
        n_done, diff_done, zd_done, h_done = (layer_sems(s) for s in ("n_done", "diff_done", "zd_done", "h_done"))
        out_transposed, out_ready = sem("out_transposed"), sem("out_ready")

        class Step:
            def __init__(self, n, it):
                self.n, self.l, self.g0 = n, *order[n]
                self.it = it
                self.g = self.g0 + 2 * it
                self.parity = self.g0 % 2
                self.pair = self.g0 // 2 + it
                self.in_loop = not isinstance(it, int)

            def before(self):
                return Step(self.n - 1, self.it) if self.n else None

        def prepared(s, it):
            return [(stage, Step(n, it)) for n in range(max(s - 3, 0), min(s + 6, STEPS))
                    for stage, slot_of in (("transpose", transpose_slot), ("aggregate", aggregate_slot)) if slot_of(n) == s]

        transpose_order = sorted(range(STEPS), key=lambda n: (transpose_slot(n), n))

        def transposed_before(st):
            i = transpose_order.index(st.n)
            return Step(transpose_order[i - 1], st.it) if i else None

        def first_steps(s, it, lead, done):
            n = s + lead
            return [Step(n, it)] if n < STEPS and order[n][0] == 0 and order[n][1] >= done else []

        def run_slots(eng, slot):
            for s in range(FIRST):
                slot(s, 0)
            with eng.Fori(0, ROUNDS) as it:
                for s in range(FIRST, FIRST + PERIOD):
                    slot(s, it)
            for s in range(AFTER, LAST):
                slot(s, 0)

        def gates(s, it):
            return [Step(s, it)] if 0 <= s < STEPS else []

        EARLY = [Step(at[(0, g)], 0) for g in range(3)]

        block = ctx.enter_context(nc.Block())

        @block.sync
        def _(sp):
            def load(g, p):
                sp.dma_start(x_all[:, bass.ts(g, COLS)].rearrange("n (b d) -> n b d", d=D),
                             x_v[:, bass.ts(g, PER), :]).then_inc(x_loaded[p], 16)
                sp.dma_start(adj_raw[p][:, :, :], adj_v[:, bass.ts(g, PER), :]).then_inc(adj_loaded[p], 16)

            def load_after(g, p):
                sp.wait_ge(stats_done, g + 1)
                sp.wait_ge(mask_done, g + 1)
                load(g + 2, p)

            def store(g, p):
                sp.wait_ge(out_ready, g + 1)
                sp.dma_start(out_v[:, bass.ts(g, PER), :], out_rows[p][:, :, :]).then_inc(stored[p], 16)

            STORES_BEHIND = 4
            for p in range(2):
                load(p, p)
            for g in range(STORES_BEHIND):
                load_after(g, g % 2)
            with sp.Fori(0, (GROUPS - 2 - STORES_BEHIND) // 2) as it:
                for p in range(2):
                    load_after(2 * it + (STORES_BEHIND + p), p)
                    store(2 * it + p, p)
            for g in range(GROUPS - 2 - STORES_BEHIND, GROUPS):
                store(g, g % 2)
            for p in range(2):
                sp.wait_ge(stored[p], 16 * (GROUPS // 2))

        @block.gpsimd
        def _(pool):
            pool.memset(ident[:, :], 0.0).then_inc(ident_zero, 1)
            pool.memset(half_power[:, :], -0.5).then_inc(power_ready, 1)
            pool.wait_ge(ident_zero, 1)
            pool.affine_select(out=ident[:, :], in_=ident[:, :], compare_op=ALU.not_equal, fill=1.0, base=0,
                               pattern=[[-1, P]], channel_multiplier=1).then_inc(ident_ready, 1)
            pool.wait_ge(power_ready, 1)

            def inverse_deviation(st):
                pool.wait_ge(var_done, st.g + 1)
                pool.tensor_tensor(rstd[st.parity][:, :], var_eps[st.parity][:, :], half_power[:, :], ALU.pow) \
                    .then_inc(rstd_done, 1)

            def difference(st):
                pool.wait_ge(n_done[st.l], st.g + 1)
                if st.l == 0:
                    pool.wait_ge(h0_done, st.g + 1)
                if st.g0 or st.in_loop:
                    pool.wait_ge(h_done[st.l], st.g)
                pool.tensor_tensor(zd[st.l][:, :], h[st.l][st.parity][:, :], n_sb[st.l][:, :], ALU.subtract) \
                    .then_inc(diff_done[st.l], 1)

            def update(st):
                pool.wait_ge(z_done[st.l], st.g + 1)
                pool.wait_ge(diff_done[st.l], st.g + 1)
                pool.tensor_tensor(zd[st.l][:, :], z_sb[st.l][:, :], zd[st.l][:, :], ALU.mult) \
                    .then_inc(zd_done[st.l], 1)

            def state_lo(st):
                pool.wait_ge(h_hi_done[st.l + 1], st.g + 1)
                pool.tensor_tensor(h_lo[st.l + 1][st.parity][:, :], h[st.l + 1][st.parity][:, :],
                                   h_hi[st.l + 1][st.parity][:, :].bitcast(f32), ALU.subtract) \
                    .then_inc(h_lo_done[st.l + 1], 1)

            def slot(s, it):
                if s == 0:
                    for st in EARLY:
                        inverse_deviation(st)
                for st in gates(s - 1, it):
                    difference(st)
                    update(st)
                for st in gates(s - 2, it):
                    if st.l < L - 1:
                        state_lo(st)
                for st in first_steps(s, it, 4, 3):
                    inverse_deviation(st)

            run_slots(pool, slot)

        @block.scalar
        def _(act):
            act.dma_start(w_nat[:, :, :], weight.rearrange("l d e -> d l e")).then_inc(w_loaded, 16)
            act.dma_start(wih_nat[:, :, :], w_ih.rearrange("(c p) e -> p c e", p=P)).then_inc(wih_loaded, 16)
            act.dma_start(whh_nat[:, :, :], w_hh.rearrange("(c p) e -> p c e", p=P)).then_inc(whh_loaded, 16)
            with nc.allow_non_contiguous_dma(reason="two columns of biases"):
                act.dma_start(bi[:, :], b_ih.rearrange("(c p) -> p c", p=P)).then_inc(b_loaded, 16)
                act.dma_start(bh[:, :], b_hh.rearrange("(c p) -> p c", p=P)).then_inc(b_loaded, 16)
            act.wait_ge(power_ready, 1)
            act.activation(warm[:, :], half_power[:, :], ACT.Sigmoid)
            act.wait_ge(wT_made, 1)
            act.copy(wT[:, :, :].rearrange("p l d -> p (l d)"), ps_wT[:, 0:L * P]).then_inc(wT_ready, 1)
            act.wait_ge(wihT_made, 1)
            act.copy(wihT[:, :], ps_wihT[:, 0:3 * P]).then_inc(wihT_ready, 1)
            act.wait_ge(whhT_made, 1)
            act.copy(whh_hi[:, :], ps_whhT[:, 0:3 * P]).then_inc(weights_hi, 1)

            def v_part_hi(l):
                act.wait_ge(v_made, l + 1)
                act.copy(v_hi[l][:, :], ps_v[l][:, 0:3 * P]).then_inc(weights_hi, 1)

            def take_transposed(st):
                act.wait_ge(transposed[st.l], st.g + 1)
                if st.l == 0:
                    if st.g0 >= 2 or st.in_loop:
                        act.wait_ge(z_made[0], st.g - 1)
                        act.wait_ge(diff_done[0], st.g - 1)
                    act.copy(h_hi[0][st.parity][:, :], ps_t[:, :]).then_inc(h_hi_done[0], 1)
                    act.copy(h[0][st.parity][:, :], ps_t[:, :]).then_inc(h0_done, 1)
                else:
                    if st.g0 or st.in_loop:
                        act.wait_ge(aggregated[st.l], st.g)
                    act.copy(nat[st.l][:, :], ps_t[:, :]).then_inc(nat_done[st.l], 1)

            def aggregate_hi(st):
                act.wait_ge(aggregated[st.l], st.g + 1)
                if st.g0 or st.in_loop:
                    act.wait_ge(z_made[st.l], st.g)
                act.copy(g_hi[st.l][:, :], ps_g[:, :]).then_inc(g_hi_done[st.l], 1)

            def reset_gate(st):
                act.wait_ge(r_made[st.l], st.g + 1)
                if st.g0 or st.in_loop:
                    act.wait_ge(rh_done[st.l], st.g)
                act.activation(r_sb[st.l][:, :], ps_r[:, :], ACT.Sigmoid, bias=b_rz[:, 0:1]).then_inc(r_done[st.l], 1)

            def update_gate(st):
                act.wait_ge(z_made[st.l], st.g + 1)
                if st.g0 or st.in_loop:
                    act.wait_ge(zd_done[st.l], st.g)
                act.activation(z_sb[st.l][:, :], ps_z[:, :], ACT.Sigmoid, bias=b_rz[:, 1:2]).then_inc(z_done[st.l], 1)

            def candidate(st):
                act.wait_ge(pre_done[st.l], st.g + 1)
                if st.g0 or st.in_loop:
                    act.wait_ge(h_done[st.l], st.g)
                act.activation(n_sb[st.l][:, :], rh[st.l][:, :], ACT.Tanh, bias=bi[:, 2:3]).then_inc(n_done[st.l], 1)

            def state_hi(st):
                act.wait_ge(h_done[st.l], st.g + 1)
                if st.g0 >= 2 or st.in_loop:
                    act.wait_ge(z_made[st.l + 1], st.g - 1)
                act.copy(h_hi[st.l + 1][st.parity][:, :], h[st.l + 1][st.parity][:, :]).then_inc(h_hi_done[st.l + 1], 1)

            def slot(s, it):
                def take(own):
                    for stage, st in prepared(s, it):
                        if (st.n == s) == own:
                            take_transposed(st) if stage == "transpose" else aggregate_hi(st)

                for st in gates(s - 1, it):
                    update_gate(st)
                take(own=True)
                if s == 0:
                    v_part_hi(0)
                    act.wait_ge(bias_ready, 1)
                for st in gates(s, it):
                    reset_gate(st)
                take(own=False)
                for st in gates(s, it):
                    candidate(st)
                for st in gates(s - 1, it):
                    if st.l < L - 1:
                        state_hi(st)
                if s + 1 in (1, 2):
                    v_part_hi(s + 1)

            run_slots(act, slot)

        @block.vector
        def _(dve):
            def mask_and_statistics(st):
                dve.wait_ge(x_loaded[st.parity], 16 * (st.pair + 1))
                for b in range(PER):
                    ins = dve.bn_stats(stats[st.parity][:, b, :], x_all[:, bass.ds(st.g * COLS + b * D, D)])
                ins.then_inc(bn_done, 1)
                dve.wait_ge(adj_loaded[st.parity], 16 * (st.pair + 1))
                dve.wait_ge(bn_done, st.g + 1)
                dve.tensor_scalar(mask_all[:, bass.ts(st.g, COLS)],
                                  adj_raw[st.parity][:, :, :].rearrange("s b t -> s (b t)"),
                                  0, None, ALU.not_equal).then_inc(mask_done, 1)
                for b in range(PER):
                    ins = dve.bn_aggr(mean_var[st.parity][:, b, :], stats[st.parity][:, b, :])
                ins.then_inc(stats_done, 1)
                dve.wait_ge(stats_done, st.g + 1)
                dve.tensor_scalar(var_eps[st.parity][:, :], mean_var[st.parity][:, :, 1], EPS, None, ALU.add) \
                    .then_inc(var_done, 1)

            def normalise(st):
                rows = relu_nat[st.parity]
                dve.wait_ge(rstd_done, st.g + 1)
                if st.g0 >= 2 or st.in_loop:
                    dve.wait_ge(aggregated[0], st.g - 1)
                    dve.wait_ge(transposed[0], st.g - 1)
                for b in range(PER):
                    ins = dve.tensor_scalar(rows[:, b * D:(b + 1) * D], x_all[:, bass.ds(st.g * COLS + b * D, D)],
                                            mean_var[st.parity][:, b, 0:1], rstd[st.parity][:, b:b + 1],
                                            ALU.subtract, ALU.mult)
                ins.then_inc(normed_done, 1)
                dve.wait_ge(normed_done, st.g + 1)
                dve.tensor_scalar(rows[:, :], rows[:, :], 0.0, None, ALU.max).then_inc(relu_done, 1)

            def first_state_lo(st):
                dve.wait_ge(h0_done, st.g + 1)
                dve.tensor_tensor(h_lo[0][st.parity][:, :], ps_t[:, :], h_hi[0][st.parity][:, :].bitcast(f32),
                                  ALU.subtract).then_inc(h_lo_done[0], 1)

            def aggregate_lo(st):
                dve.wait_ge(g_hi_done[st.l], st.g + 1)
                dve.tensor_tensor(g_lo[st.l][:, :], ps_g[:, :], g_hi[st.l][:, :].bitcast(f32), ALU.subtract) \
                    .then_inc(g_lo_done[st.l], 1)

            def reset_product(st):
                dve.wait_ge(hn_made[st.l], st.g + 1)
                dve.wait_ge(r_done[st.l], st.g + 1)
                if st.g0 or st.in_loop:
                    dve.wait_ge(n_done[st.l], st.g)
                dve.scalar_tensor_tensor(out=rh[st.l][:, :], in0=ps_hn[:, :], scalar=bh[:, 2:3], in1=r_sb[st.l][:, :],
                                         op0=ALU.add, op1=ALU.mult).then_inc(rh_done[st.l], 1)

            def candidate_input(st):
                dve.wait_ge(in_made[st.l], st.g + 1)
                dve.wait_ge(rh_done[st.l], st.g + 1)
                dve.tensor_tensor(rh[st.l][:, :], ps_in[:, :], rh[st.l][:, :], ALU.add).then_inc(pre_done[st.l], 1)

            def new_state(st):
                dve.wait_ge(zd_done[st.l], st.g + 1)
                dve.tensor_tensor(h[st.l + 1][st.parity][:, :], n_sb[st.l][:, :], zd[st.l][:, :], ALU.add) \
                    .then_inc(h_done[st.l], 1)

            def residual(st):
                dve.wait_ge(out_transposed, st.g + 1)
                if st.g0 >= 2 or st.in_loop:
                    dve.wait_ge(stored[st.parity], 16 * st.pair)
                dve.tensor_tensor(out_rows[st.parity][:, :, :].rearrange("n b d -> n (b d)"), ps_out[:, :],
                                  x_all[:, bass.ts(st.g, COLS)], ALU.add).then_inc(out_ready, 1)

            mask_and_statistics(EARLY[0])
            mask_and_statistics(EARLY[1])
            normalise(EARLY[0])
            dve.wait_ge(weights_hi, 1)
            dve.tensor_tensor(whh_lo[:, :], ps_whhT[:, 0:3 * P], whh_hi[:, :].bitcast(f32), ALU.subtract) \
                .then_inc(weights_lo, 1)
            normalise(EARLY[1])
            dve.wait_ge(b_loaded, 32)
            dve.tensor_tensor(b_rz[:, :], bi[:, 0:2], bh[:, 0:2], ALU.add).then_inc(bias_ready, 1)

            def v_part_lo(l):
                dve.wait_ge(weights_hi, l + 2)
                dve.tensor_tensor(v_lo[l][:, :], ps_v[l][:, 0:3 * P], v_hi[l][:, :].bitcast(f32), ALU.subtract) \
                    .then_inc(weights_lo, 1)

            def slot(s, it):
                for stage, st in prepared(s, it):
                    if st.n == s and stage == "aggregate":
                        aggregate_lo(st)
                    elif st.n == s and st.l == 0:
                        first_state_lo(st)
                if s == 0:
                    v_part_lo(0)
                    mask_and_statistics(EARLY[2])
                    normalise(EARLY[2])
                for st in first_steps(s, it, 4, 3):
                    mask_and_statistics(st)
                for st in first_steps(s, it, 3, 3):
                    normalise(st)
                for st in gates(s, it):
                    reset_product(st)
                for stage, st in prepared(s, it):
                    if st.n > s and stage == "aggregate":
                        aggregate_lo(st)
                for st in gates(s, it):
                    candidate_input(st)
                for st in gates(s - 1, it):
                    new_state(st)
                for stage, st in prepared(s, it):
                    if st.n > s and stage == "transpose" and st.l == 0:
                        first_state_lo(st)
                for st in gates(s - 2, it):
                    if st.l == L - 1:
                        residual(st)
                if s + 1 in (1, 2):
                    v_part_lo(s + 1)

            run_slots(dve, slot)

        @block.tensor
        def _(pe):
            def transpose4(dst, src):
                for b in range(PER):
                    ins = pe.transpose(dst[:, b * P:(b + 1) * P], src[:, b * P:(b + 1) * P], ident[:, :])
                return ins

            def transpose_state(st):
                if st.l == 0:
                    src = relu_nat[st.parity]
                    pe.wait_ge(relu_done, st.g + 1)
                else:
                    src = h[st.l][st.parity]
                    pe.wait_ge(h_done[st.l - 1], st.g + 1)
                last = transposed_before(st)
                if last and last.l == 0:
                    pe.wait_ge(h_lo_done[0], last.g + 1)
                elif last:
                    pe.wait_ge(nat_done[last.l], last.g + 1)
                transpose4(ps_t, src).then_inc(transposed[st.l], 1)

            def transpose_out(st):
                pe.wait_ge(h_done[L - 1], st.g + 1)
                if st.g0 or st.in_loop:
                    pe.wait_ge(out_ready, st.g)
                transpose4(ps_out, h[L][st.parity]).then_inc(out_transposed, 1)

            def aggregate(st):
                if st.l == 0:
                    rows = relu_nat[st.parity]
                    pe.wait_ge(relu_done, st.g + 1)
                    pe.wait_ge(mask_done, st.g + 1)
                else:
                    rows = nat[st.l]
                    pe.wait_ge(nat_done[st.l], st.g + 1)
                last = st.before()
                if last:
                    pe.wait_ge(g_lo_done[last.l], last.g + 1)
                for b in range(PER):
                    cols = slice(b * P, (b + 1) * P)
                    ins = pe.matmul(ps_g[:, cols], rows[:, cols], mask_all[:, bass.ds(st.g * COLS + b * N, N)],
                                    start=True, stop=True)
                ins.then_inc(aggregated[st.l], 1)

            def product(ps, w_hi, w_lo, gate, a_hi, a_lo, start, stop):
                cols = slice(gate * P, (gate + 1) * P)
                pe.matmul(ps[:, :], w_hi[:, cols], a_hi[:, :], start=start, stop=False)
                pe.matmul(ps[:, :], w_hi[:, cols], a_lo[:, :], start=False, stop=False)
                return pe.matmul(ps[:, :], w_lo[:, cols], a_hi[:, :], start=False, stop=stop)

            def state_part(st, ps, gate, stop):
                return product(ps, whh_hi, whh_lo, gate, h_hi[st.l][st.parity], h_lo[st.l][st.parity], True, stop)

            def aggregate_part(st, ps, gate, start):
                return product(ps, v_hi[st.l], v_lo[st.l], gate, g_hi[st.l], g_lo[st.l], start, True)

            def hidden_candidate(st):
                pe.wait_ge(h_hi_done[st.l], st.g + 1)
                pe.wait_ge(h_lo_done[st.l], st.g + 1)
                last = st.before()
                if last:
                    pe.wait_ge(rh_done[last.l], last.g + 1)
                state_part(st, ps_hn, 2, True).then_inc(hn_made[st.l], 1)

            def reset(st):
                last = st.before()
                if last:
                    pe.wait_ge(r_done[last.l], last.g + 1)
                state_part(st, ps_r, 0, False)
                pe.wait_ge(g_hi_done[st.l], st.g + 1)
                pe.wait_ge(g_lo_done[st.l], st.g + 1)
                aggregate_part(st, ps_r, 0, False).then_inc(r_made[st.l], 1)

            def input_candidate(st):
                last = st.before()
                if last:
                    pe.wait_ge(pre_done[last.l], last.g + 1)
                aggregate_part(st, ps_in, 2, True).then_inc(in_made[st.l], 1)

            def update(st):
                last = st.before()
                if last:
                    pe.wait_ge(z_done[last.l], last.g + 1)
                state_part(st, ps_z, 1, False)
                aggregate_part(st, ps_z, 1, False).then_inc(z_made[st.l], 1)

            pe.wait_ge(ident_ready, 1)
            pe.wait_ge(w_loaded, 16)
            for l in range(L):
                ins = pe.transpose(ps_wT[:, l * P:(l + 1) * P], w_nat[:, l, :], ident[:, :])
            ins.then_inc(wT_made, 1)
            pe.wait_ge(wih_loaded, 16)
            for c in range(3):
                ins = pe.transpose(ps_wihT[:, c * P:(c + 1) * P], wih_nat[:, c, :], ident[:, :])
            ins.then_inc(wihT_made, 1)
            pe.wait_ge(whh_loaded, 16)
            for c in range(3):
                ins = pe.transpose(ps_whhT[:, c * P:(c + 1) * P], whh_nat[:, c, :], ident[:, :])
            ins.then_inc(whhT_made, 1)
            pe.wait_ge(wT_ready, 1)
            pe.wait_ge(wihT_ready, 1)

            def make_v(l):
                if l == 2:
                    pe.wait_ge(weights_lo, 2)
                pe.matmul(ps_v[l][:, 0:3 * P], wT[:, l, :], wihT[:, :], start=True, stop=True).then_inc(v_made, 1)

            make_v(0)

            def slot(s, it):
                def prepare(own):
                    for stage, st in prepared(s, it):
                        if (st.n == s) == own:
                            transpose_state(st) if stage == "transpose" else aggregate(st)

                prepare(own=True)
                for st in gates(s, it):
                    if s < FIRST and st.g0 == 0:
                        pe.wait_ge(weights_lo, st.l + 2)
                    hidden_candidate(st)
                    reset(st)
                prepare(own=False)
                for st in gates(s - 2, it):
                    if st.l == L - 1:
                        transpose_out(st)
                for st in gates(s, it):
                    input_candidate(st)
                    update(st)
                if s + 1 in (1, 2):
                    make_v(s + 1)

            run_slots(pe, slot)


_INS = ["x", "adj", "L0_gnn_weight", "L0_gnn_w_ih", "L0_gnn_w_hh", "L0_gnn_b_ih", "L0_gnn_b_hh"]
_OUTS = [((64, 128, 128), "float32")]


def kernel(**inputs):
    import numpy as _np
    import concourse.bacc as _bacc
    from concourse import mybir as _mybir
    from concourse.bass_utils import run_bass_kernel_spmd as _run

    nc = _bacc.Bacc("TRN2", target_bir_lowering=False, num_devices=1)
    arrays, args = {}, []
    for name in _INS:
        a = _np.ascontiguousarray(inputs[name])
        arrays[f"in_{name}_dram"] = a
        args.append(nc.dram_tensor(f"in_{name}_dram", a.shape, _mybir.dt.from_np(a.dtype), kind="ExternalInput").ap())
    for i, (shape, dtype) in enumerate(_OUTS):
        dt = _mybir.dt.from_np(_np.dtype(dtype))
        args.append(nc.dram_tensor(f"out_{i}_dram", shape, dt, kind="ExternalOutput").ap())
    gnn_residual_kernel(nc, *args)
    r = _run(nc, [arrays], core_ids=[0])
    return r.results[0]["out_0_dram"]
```

```python
from contextlib import ExitStack

import concourse.bass as bass
from concourse import mybir


def gnn_residual_kernel(nc, x, adj, weight, w_ih, w_hh, b_ih, b_hh, out):
    f32, f32r, i32 = mybir.dt.float32, mybir.dt.float32r, mybir.dt.int32
    ALU = mybir.AluOpType
    ACT = mybir.ActivationFunctionType

    B, N, D = x.shape
    L = weight.shape[0]
    P = 128
    assert N == P and D == P and L == 3
    PER = 4
    COLS = PER * N
    GROUPS = B // PER
    EPS = 1e-5

    order = [(0, 0), (0, 1), (0, 2), (1, 0), (1, 1), (0, 3), (2, 0), (1, 2), (2, 1)]
    for i in range(4, GROUPS - 2):
        order += [(l, i - l) for l in range(L)]
    F = GROUPS - 1
    order += [(0, F - 1), (1, F - 2), (0, F), (2, F - 3), (1, F - 1), (1, F), (2, F - 2), (2, F - 1), (2, F)]
    STEPS = len(order)
    at = {s: n for n, s in enumerate(order)}
    assert STEPS == L * GROUPS

    def transpose_slot(n):
        l, g = order[n]
        made = at[(l - 1, g)] if l else max(g - 3, -2)
        return max(n - 2, made + 2)

    def aggregate_slot(n):
        return max(transpose_slot(n) if order[n][0] else 0, n - 1)

    FIRST = 3 * L + 2
    RING = 3
    PERIOD = 2 * L
    ROUNDS = (STEPS - 10 - FIRST) // PERIOD
    AFTER = FIRST + ROUNDS * PERIOD
    LAST = STEPS + 2

    x_v = x.rearrange("b n d -> n b d")
    adj_v = adj.rearrange("b s t -> s b t")
    out_v = out.rearrange("b n d -> n b d")

    ctx = ExitStack()
    with ctx:
        def sb(name, shape, dt=f32):
            return ctx.enter_context(nc.sbuf_tensor(name, shape, dt))

        def sem(name):
            return ctx.enter_context(nc.semaphore(name))

        def layer_sems(name):
            return [sem(f"{name}_{l}") for l in range(L)]

        x_all = sb("x_all", [P, B * D])
        mask_all = sb("mask_all", [P, B * N])
        adj_raw = [sb(f"adj_raw{p}", [P, PER, N], i32) for p in range(2)]
        out_rows = [sb(f"out_rows{p}", [P, PER, D]) for p in range(2)]
        ident = sb("ident", [P, P])
        w_nat = sb("w_nat", [P, L, P])
        wih_nat = sb("wih_nat", [P, 3, P])
        whh_nat = sb("whh_nat", [P, 3, P])
        wT = sb("wT", [P, L, P])
        wihT = sb("wihT", [P, 3 * P])
        v_hi = [sb(f"v_hi{l}", [P, 3 * P], f32r) for l in range(L)]
        v_lo = [sb(f"v_lo{l}", [P, 3 * P], f32r) for l in range(L)]
        whh_hi = sb("whh_hi", [P, 3 * P], f32r)
        whh_lo = sb("whh_lo", [P, 3 * P], f32r)
        bi = sb("bi", [P, 3])
        bh = sb("bh", [P, 3])
        b_rz = sb("b_rz", [P, 2])
        half_power = sb("half_power", [P, PER])
        minus_mean = [sb(f"minus_mean{p}", [P, PER]) for p in range(2)]
        warm = sb("warm", [P, PER])
        stats = [sb(f"stats{p}", [P, PER, 6]) for p in range(2)]
        mean_var = [sb(f"mean_var{p}", [P, PER, 2]) for p in range(2)]
        var_eps = [sb(f"var_eps{p}", [P, PER]) for p in range(2)]
        rstd = [sb(f"rstd{p}", [P, PER]) for p in range(2)]
        relu_nat = [sb(f"relu_nat{p}", [P, COLS]) for p in range(2)]
        nat = [sb(f"nat{k}", [P, COLS]) for k in range(RING)]
        g_hi = [sb(f"g_hi{k}", [P, COLS], f32r) for k in range(RING)]
        g_lo = [sb(f"g_lo{k}", [P, COLS], f32r) for k in range(RING)]
        r_sb = [sb(f"r{k}", [P, COLS]) for k in range(RING)]
        z_sb = [sb(f"z{k}", [P, COLS]) for k in range(RING)]
        rh = [sb(f"rh{k}", [P, COLS]) for k in range(RING)]
        n_sb = [sb(f"n{k}", [P, COLS]) for k in range(RING)]
        zd = [sb(f"zd{k}", [P, COLS]) for k in range(RING)]
        h = [[sb(f"h{l}_{p}", [P, COLS]) for p in range(2)] for l in range(L + 1)]
        h_hi = [[sb(f"h_hi{l}_{p}", [P, COLS], f32r) for p in range(2)] for l in range(L)]
        h_lo = [[sb(f"h_lo{l}_{p}", [P, COLS], f32r) for p in range(2)] for l in range(L)]
        h_spare = sb("h_spare", [P, COLS])

        def bank(name):
            return ctx.enter_context(nc.psum_tensor(name, [P, COLS], f32))

        ps_t = [bank("ps_t0"), bank("ps_t1")]
        ps_out, ps_g, ps_hn, ps_r, ps_in, ps_z = (bank(f"ps_{b}") for b in ("out", "g", "hn", "r", "in", "z"))
        ps_whhT, ps_wihT, ps_wT, ps_v = ps_hn, ps_r, ps_in, [ps_z, ps_out, ps_out]

        x_loaded = [sem(f"x_loaded{p}") for p in range(2)]
        adj_loaded = [sem(f"adj_loaded{p}") for p in range(2)]
        stored = [sem(f"stored{p}") for p in range(2)]
        final_stored = sem("final_stored")
        w_loaded, wih_loaded, whh_loaded, b_loaded = sem("w_loaded"), sem("wih_loaded"), sem("whh_loaded"), sem("b_loaded")
        ident_zero, ident_ready, power_ready = sem("ident_zero"), sem("ident_ready"), sem("power_ready")
        wT_made, wihT_made, whhT_made, v_made = sem("wT_made"), sem("wihT_made"), sem("whhT_made"), sem("v_made")
        wT_ready, wihT_ready, bias_ready = sem("wT_ready"), sem("wihT_ready"), sem("bias_ready")
        weights_hi, weights_lo = sem("weights_hi"), sem("weights_lo")
        bn_done, stats_done, var_done, rstd_done = sem("bn_done"), sem("stats_done"), sem("var_done"), sem("rstd_done")
        mean_negated, centred, relu_done, h0_done = sem("mean_negated"), sem("centred"), sem("relu_done"), sem("h0_done")
        mask_done, early_mask_done = sem("mask_done"), sem("early_mask_done")
        transposed = layer_sems("transposed")
        nat_done = layer_sems("nat_done")
        h_hi_done, h_lo_done = layer_sems("h_hi_done"), layer_sems("h_lo_done")
        aggregated = layer_sems("aggregated")
        g_hi_done, g_lo_done = layer_sems("g_hi_done"), layer_sems("g_lo_done")
        hn_made, r_made, in_made, z_made = (layer_sems(s) for s in ("hn_made", "r_made", "in_made", "z_made"))
        r_done, z_done, rh_done, pre_done = (layer_sems(s) for s in ("r_done", "z_done", "rh_done", "pre_done"))
        n_done, diff_done, zd_done, h_done = (layer_sems(s) for s in ("n_done", "diff_done", "zd_done", "h_done"))
        out_transposed, out_ready = sem("out_transposed"), sem("out_ready")
        rows_copied, late_out_ready = sem("rows_copied"), sem("late_out_ready")

        class Step:
            def __init__(self, n, it):
                self.n, self.l, self.g0 = n, *order[n]
                self.it = it
                self.g = self.g0 + 2 * it
                self.parity = self.g0 % 2
                self.pair = self.g0 // 2 + it
                self.in_loop = not isinstance(it, int)
                self.ring = n % RING

            def user(self):
                return [Step(self.n - RING, self.it)] if self.n >= RING else []

            def before(self):
                return Step(self.n - 1, self.it) if self.n else None

        def prepared(s, it, stage, when):
            def time(n):
                if n == s:
                    return "own"
                return "early" if stage == "transpose" and aggregate_slot(n) == s else "late"

            slot_of = transpose_slot if stage == "transpose" else aggregate_slot
            return [Step(n, it) for n in range(max(s - 3, 0), min(s + 6, STEPS)) if slot_of(n) == s and time(n) == when]

        def transposed_before(st):
            return Step(st.n - 2, st.it) if st.n >= 2 else None

        def first_steps(s, it, lead, done):
            n = s + lead
            return [Step(n, it)] if n < STEPS and order[n][0] == 0 and order[n][1] >= done else []

        def run_slots(eng, slot):
            for s in range(FIRST):
                slot(s, 0)
            with eng.Fori(0, ROUNDS) as it:
                for s in range(FIRST, FIRST + PERIOD):
                    slot(s, it)
            for s in range(AFTER, LAST):
                slot(s, 0)

        SPARE = [(1, 2), (2, F)]

        def state(l, st):
            return h_spare if (l, st.g0) in SPARE and not st.in_loop else h[l][st.parity]

        def gates(s, it):
            return [Step(s, it)] if 0 <= s < STEPS else []

        def soon(st):
            return not st.in_loop and any(user.l == st.l + 1 and user.g0 == st.g0
                                          for user in prepared(st.n + 2, 0, "transpose", "early"))

        FINAL = Step(STEPS - 1, 0)
        HALVES = [slice(k * COLS // 2, (k + 1) * COLS // 2) for k in range(2)]
        Z_BANKS, OUT_BANKS = [ps_z, ps_g], [ps_hn, ps_in]
        final_rows = relu_nat[0]

        EARLY = [Step(at[(0, g)], 0) for g in range(3)]
        V_MADE = {0: 1, 3: 2}
        V_TAKEN = {2: 1, 4: 2}

        def wait_for_mask(eng, g):
            if isinstance(g, int) and g in (1, 2):
                eng.wait_ge(early_mask_done, g)
            else:
                eng.wait_ge(mask_done, g + 1)

        block = ctx.enter_context(nc.Block())

        @block.sync
        def _(sp):
            def load_x(g, p):
                sp.dma_start(x_all[:, bass.ts(g, COLS)].rearrange("n (b d) -> n b d", d=D),
                             x_v[:, bass.ts(g, PER), :]).then_inc(x_loaded[p], 16)

            def load_adj(g, p):
                sp.dma_start(adj_raw[p][:, :, :], adj_v[:, bass.ts(g, PER), :]).then_inc(adj_loaded[p], 16)

            def load_after(g, p):
                sp.wait_ge(stats_done, g + 1)
                wait_for_mask(sp, g)
                load_x(g + 2, p)
                load_adj(g + 2, p)

            def store(g, p):
                sp.wait_ge(out_ready, g + 1)
                store_rows(g, p)

            def store_rows(g, p):
                sp.dma_start(out_v[:, bass.ts(g, PER), :], out_rows[p][:, :, :]).then_inc(stored[p], 16)

            STORES_BEHIND = 4
            load_x(0, 0)
            sp.dma_start(w_nat[:, :, :], weight.rearrange("l d e -> d l e")).then_inc(w_loaded, 16)
            load_adj(0, 0)
            load_x(1, 1)
            load_adj(1, 1)
            with nc.allow_non_contiguous_dma(reason="columns of biases"):
                sp.dma_start(bi[:, :], b_ih.rearrange("(c p) -> p c", p=P)).then_inc(b_loaded, 16)
                sp.dma_start(bh[:, :], b_hh.rearrange("(c p) -> p c", p=P)).then_inc(b_loaded, 16)
            for g in range(STORES_BEHIND):
                load_after(g, g % 2)
            with sp.Fori(0, (GROUPS - 2 - STORES_BEHIND) // 2) as it:
                for p in range(2):
                    load_after(2 * it + (STORES_BEHIND + p), p)
                    store(2 * it + p, p)
            for g in range(GROUPS - 2 - STORES_BEHIND, F - 2):
                store(g, g % 2)
            for k, g in enumerate((F - 2, F - 1)):
                sp.wait_ge(late_out_ready, k + 1)
                store_rows(g, g % 2)
            sp.wait_ge(out_ready, F)
            sp.dma_start(out_v[:, F * PER:, :],
                         final_rows[:, :].rearrange("n (b d) -> n b d", d=D)).then_inc(final_stored, 16)
            sp.wait_ge(stored[0], 16 * (GROUPS // 2))
            sp.wait_ge(stored[1], 16 * (GROUPS // 2 - 1))
            sp.wait_ge(final_stored, 16)

        @block.gpsimd
        def _(pool):
            pool.memset(ident[:, :], 0.0).then_inc(ident_zero, 1)
            pool.memset(half_power[:, :], -0.5).then_inc(power_ready, 1)
            pool.wait_ge(ident_zero, 1)
            pool.affine_select(out=ident[:, :], in_=ident[:, :], compare_op=ALU.not_equal, fill=1.0, base=0,
                               pattern=[[-1, P]], channel_multiplier=1).then_inc(ident_ready, 1)
            pool.wait_ge(power_ready, 1)

            def inverse_deviation(st):
                pool.wait_ge(var_done, st.g + 1)
                pool.tensor_tensor(rstd[st.parity][:, :], var_eps[st.parity][:, :], half_power[:, :], ALU.pow) \
                    .then_inc(rstd_done, 1)

            def first_state(st):
                pool.wait_ge(h_lo_done[0], st.g + 1)
                if st.g0 >= 2 or st.in_loop:
                    pool.wait_ge(diff_done[0], st.g - 1)
                pool.tensor_tensor(h[0][st.parity][:, :], h_hi[0][st.parity][:, :].bitcast(f32),
                                   h_lo[0][st.parity][:, :].bitcast(f32), ALU.add).then_inc(h0_done, 1)

            def difference(st):
                pool.wait_ge(n_done[st.l], st.g + 1)
                if st.l == 0:
                    pool.wait_ge(h0_done, st.g + 1)
                for last in st.user():
                    pool.wait_ge(h_done[last.l], last.g + 1)
                pool.tensor_tensor(zd[st.ring][:, :], state(st.l, st)[:, :], n_sb[st.ring][:, :], ALU.subtract) \
                    .then_inc(diff_done[st.l], 1)

            def update(st):
                pool.wait_ge(z_done[st.l], st.g + 1)
                pool.wait_ge(diff_done[st.l], st.g + 1)
                pool.tensor_tensor(zd[st.ring][:, :], z_sb[st.ring][:, :], zd[st.ring][:, :], ALU.mult) \
                    .then_inc(zd_done[st.l], 1)

            def state_lo(st):
                pool.wait_ge(h_hi_done[st.l + 1], st.g + 1)
                pool.tensor_tensor(h_lo[st.l + 1][st.parity][:, :], state(st.l + 1, st)[:, :],
                                   h_hi[st.l + 1][st.parity][:, :].bitcast(f32), ALU.subtract) \
                    .then_inc(h_lo_done[st.l + 1], 1)

            def mask(st):
                pool.wait_ge(adj_loaded[st.parity], 16 * (st.pair + 1))
                pool.tensor_scalar(mask_all[:, bass.ts(st.g, COLS)],
                                   adj_raw[st.parity][:, :, :].rearrange("s b t -> s (b t)"),
                                   0, 0, ALU.is_equal, ALU.is_equal).then_inc(early_mask_done, 1)

            def late_residual(st):
                pool.wait_ge(rows_copied, st.g - (F - 3))
                rows = out_rows[st.parity][:, :, :].rearrange("n b d -> n (b d)")
                pool.tensor_tensor(rows, rows, x_all[:, bass.ts(st.g, COLS)], ALU.add).then_inc(late_out_ready, 1)

            def slot(s, it):
                if s == 0:
                    inverse_deviation(EARLY[0])
                    inverse_deviation(EARLY[1])
                    mask(EARLY[1])
                    mask(EARLY[2])
                    inverse_deviation(EARLY[2])
                made = [st for st in gates(s - 2, it) if st.l < L - 1]
                for st in gates(s - 1, it):
                    if st.n != FINAL.n:
                        difference(st)
                        for new in made:
                            if soon(new):
                                state_lo(new)
                        update(st)
                for new in made:
                    if not soon(new):
                        state_lo(new)
                if s in (FINAL.n, FINAL.n + 1):
                    late_residual(Step(s - 2, it))
                for when in ("own", "early", "late"):
                    for st in prepared(s, it, "transpose", when):
                        if st.l == 0:
                            first_state(st)
                for st in first_steps(s, it, 4, 3):
                    inverse_deviation(st)

            run_slots(pool, slot)

        @block.scalar
        def _(act):
            act.dma_start(whh_nat[:, :, :], w_hh.rearrange("(c p) e -> p c e", p=P)).then_inc(whh_loaded, 16)
            act.dma_start(wih_nat[:, :, :], w_ih.rearrange("(c p) e -> p c e", p=P)).then_inc(wih_loaded, 16)
            act.wait_ge(power_ready, 1)
            act.activation(warm[:, :], half_power[:, :], ACT.Sigmoid)
            act.wait_ge(whhT_made, 1)
            act.copy(whh_hi[:, :], ps_whhT[:, 0:3 * P]).then_inc(weights_hi, 1)
            act.wait_ge(wT_made, 1)
            act.copy(wT[:, :, :].rearrange("p l d -> p (l d)"), ps_wT[:, 0:L * P]).then_inc(wT_ready, 1)
            act.wait_ge(wihT_made, 1)
            act.copy(wihT[:, :], ps_wihT[:, 0:3 * P]).then_inc(wihT_ready, 1)

            def v_part_hi(l):
                act.wait_ge(v_made, l + 1)
                act.copy(v_hi[l][:, :], ps_v[l][:, 0:3 * P]).then_inc(weights_hi, 1)

            def centre(st):
                act.wait_ge(mean_negated, st.g)
                if st.g0 >= 2:
                    act.wait_ge(aggregated[0], st.g - 1)
                    act.wait_ge(transposed[0], st.g - 1)
                for b in range(PER):
                    ins = act.activation(relu_nat[st.parity][:, b * D:(b + 1) * D],
                                         x_all[:, st.g * COLS + b * D:st.g * COLS + (b + 1) * D], ACT.Relu,
                                         bias=minus_mean[st.parity][:, b:b + 1])
                ins.then_inc(centred, 1)

            def take_transposed(st):
                act.wait_ge(transposed[st.l], st.g + 1)
                if st.l == 0:
                    if st.g0 >= 2 or st.in_loop:
                        act.wait_ge(z_made[0], st.g - 1)
                        act.wait_ge(h0_done, st.g - 1)
                    act.copy(h_hi[0][st.parity][:, :], ps_t[st.n % 2][:, :]).then_inc(h_hi_done[0], 1)
                else:
                    for last in st.user():
                        act.wait_ge(aggregated[last.l], last.g + 1)
                    act.copy(nat[st.ring][:, :], ps_t[st.n % 2][:, :]).then_inc(nat_done[st.l], 1)

            def aggregate_hi(st):
                act.wait_ge(aggregated[st.l], st.g + 1)
                for last in st.user():
                    act.wait_ge(z_made[last.l], last.g + 1)
                act.copy(g_hi[st.ring][:, :], ps_g[:, :]).then_inc(g_hi_done[st.l], 1)

            def reset_gate(st):
                act.wait_ge(r_made[st.l], st.g + 1)
                for last in st.user():
                    act.wait_ge(rh_done[last.l], last.g + 1)
                act.activation(r_sb[st.ring][:, :], ps_r[:, :], ACT.Sigmoid, bias=b_rz[:, 0:1]).then_inc(r_done[st.l], 1)

            def update_gate(st):
                act.wait_ge(z_made[st.l], st.g + 1)
                for last in st.user():
                    act.wait_ge(zd_done[last.l], last.g + 1)
                act.activation(z_sb[st.ring][:, :], ps_z[:, :], ACT.Sigmoid, bias=b_rz[:, 1:2]).then_inc(z_done[st.l], 1)

            def final_update_gate(st):
                for k, cols in enumerate(HALVES):
                    act.wait_ge(z_made[st.l], st.g + 1 + k)
                    act.activation(z_sb[st.ring][:, cols], Z_BANKS[k][:, cols], ACT.Sigmoid, bias=b_rz[:, 1:2]) \
                        .then_inc(z_done[st.l], 1)

            def copy_rows(st):
                act.wait_ge(out_transposed, st.g + 1)
                act.wait_ge(stored[st.parity], 16 * st.pair)
                act.copy(out_rows[st.parity][:, :, :].rearrange("n b d -> n (b d)"), ps_out[:, :]).then_inc(rows_copied, 1)

            def candidate(st):
                act.wait_ge(pre_done[st.l], st.g + 1)
                for last in st.user():
                    act.wait_ge(h_done[last.l], last.g + 1)
                act.activation(n_sb[st.ring][:, :], rh[st.ring][:, :], ACT.Tanh, bias=bi[:, 2:3]).then_inc(n_done[st.l], 1)

            def final_candidate(st):
                for k, cols in enumerate(HALVES):
                    act.wait_ge(pre_done[st.l], st.g + 1 + k)
                    act.activation(n_sb[st.ring][:, cols], rh[st.ring][:, cols], ACT.Tanh, bias=bi[:, 2:3]) \
                        .then_inc(n_done[st.l], 1)

            def state_hi(st):
                act.wait_ge(h_done[st.l], st.g + 1)
                if st.g0 >= 2 or st.in_loop:
                    act.wait_ge(z_made[st.l + 1], st.g - 1)
                act.copy(h_hi[st.l + 1][st.parity][:, :], state(st.l + 1, st)[:, :]).then_inc(h_hi_done[st.l + 1], 1)

            def slot(s, it):
                for when in ("own", "early"):
                    for st in prepared(s, it, "transpose", when):
                        if s or when == "own":
                            take_transposed(st)
                for st in gates(s - 2, it):
                    if soon(st):
                        state_hi(st)
                for st in gates(s - 1, it):
                    if st.n == FINAL.n:
                        final_update_gate(st)
                    else:
                        update_gate(st)
                for st in prepared(s, it, "aggregate", "own"):
                    aggregate_hi(st)
                if s == 0:
                    v_part_hi(0)
                    centre(EARLY[1])
                    act.wait_ge(bias_ready, 1)
                for st in gates(s, it):
                    reset_gate(st)
                if s in (FINAL.n, FINAL.n + 1):
                    copy_rows(Step(s - 2, it))
                if s == 0:
                    for st in prepared(s, it, "transpose", "early"):
                        take_transposed(st)
                for st in prepared(s, it, "aggregate", "late"):
                    aggregate_hi(st)
                if s == 0:
                    centre(EARLY[2])
                for st in prepared(s, it, "transpose", "late"):
                    take_transposed(st)
                for st in gates(s, it):
                    if st.n == FINAL.n:
                        final_candidate(st)
                    else:
                        candidate(st)
                for st in gates(s - 1, it):
                    if st.l < L - 1 and not soon(st):
                        state_hi(st)
                if s in V_TAKEN:
                    v_part_hi(V_TAKEN[s])

            run_slots(act, slot)

        @block.vector
        def _(dve):
            def row_statistics(st):
                dve.wait_ge(x_loaded[st.parity], 16 * (st.pair + 1))
                for b in range(PER):
                    ins = dve.bn_stats(stats[st.parity][:, b, :], x_all[:, bass.ds(st.g * COLS + b * D, D)])
                ins.then_inc(bn_done, 1)

            def mask(st):
                dve.wait_ge(adj_loaded[st.parity], 16 * (st.pair + 1))
                if st.in_loop:
                    dve.wait_ge(bn_done, st.g + 1)
                dve.tensor_scalar(mask_all[:, bass.ts(st.g, COLS)],
                                  adj_raw[st.parity][:, :, :].rearrange("s b t -> s (b t)"),
                                  0, None, ALU.not_equal) \
                    .then_inc(mask_done, 3 if not st.in_loop and st.g == 3 else 1)

            def aggregate_statistics(st):
                if not st.in_loop:
                    dve.wait_ge(bn_done, st.g + 1)
                for b in range(PER):
                    ins = dve.bn_aggr(mean_var[st.parity][:, b, :], stats[st.parity][:, b, :])
                ins.then_inc(stats_done, 1)
                dve.wait_ge(stats_done, st.g + 1)
                dve.tensor_scalar(var_eps[st.parity][:, :], mean_var[st.parity][:, :, 1], EPS, None, ALU.add) \
                    .then_inc(var_done, 1)

            def negate_mean(st):
                dve.tensor_scalar(minus_mean[st.parity][:, :], mean_var[st.parity][:, :, 0], -1.0, None, ALU.mult) \
                    .then_inc(mean_negated, 1)

            def centre(st):
                if st.g0 >= 2 or st.in_loop:
                    dve.wait_ge(aggregated[0], st.g - 1)
                    dve.wait_ge(transposed[0], st.g - 1)
                for b in range(PER):
                    ins = dve.tensor_scalar(relu_nat[st.parity][:, b * D:(b + 1) * D],
                                            x_all[:, bass.ds(st.g * COLS + b * D, D)],
                                            mean_var[st.parity][:, b, 0:1], 0.0, ALU.subtract, ALU.max)
                ins.then_inc(centred, 1)

            def scale(st):
                rows = relu_nat[st.parity][:, :].rearrange("n (b d) -> n b d", d=D)
                dve.wait_ge(centred, st.g + 1)
                dve.wait_ge(rstd_done, st.g + 1)
                dve.tensor_tensor(rows, rows, rstd[st.parity][:, :].unsqueeze(2).broadcast_to([P, PER, D]), ALU.mult) \
                    .then_inc(relu_done, 1)

            def first_state_lo(st):
                dve.wait_ge(h_hi_done[0], st.g + 1)
                if st.g0 >= 2 or st.in_loop:
                    dve.wait_ge(h0_done, st.g - 1)
                dve.tensor_tensor(h_lo[0][st.parity][:, :], ps_t[st.n % 2][:, :], h_hi[0][st.parity][:, :].bitcast(f32),
                                  ALU.subtract).then_inc(h_lo_done[0], 1)

            def aggregate_lo(st):
                dve.wait_ge(g_hi_done[st.l], st.g + 1)
                dve.tensor_tensor(g_lo[st.ring][:, :], ps_g[:, :], g_hi[st.ring][:, :].bitcast(f32), ALU.subtract) \
                    .then_inc(g_lo_done[st.l], 1)

            def reset_product(st):
                dve.wait_ge(hn_made[st.l], st.g + 1)
                dve.wait_ge(r_done[st.l], st.g + 1)
                for last in st.user():
                    dve.wait_ge(n_done[last.l], last.g + 1)
                dve.scalar_tensor_tensor(out=rh[st.ring][:, :], in0=ps_hn[:, :], scalar=bh[:, 2:3], in1=r_sb[st.ring][:, :],
                                         op0=ALU.add, op1=ALU.mult).then_inc(rh_done[st.l], 1)

            def candidate_input(st):
                dve.wait_ge(in_made[st.l], st.g + 1)
                dve.wait_ge(rh_done[st.l], st.g + 1)
                dve.tensor_tensor(rh[st.ring][:, :], ps_in[:, :], rh[st.ring][:, :], ALU.add).then_inc(pre_done[st.l], 1)

            def new_state(st):
                dve.wait_ge(zd_done[st.l], st.g + 1)
                if st.l < L - 1 and st.g0 >= 2 and not st.in_loop and (st.l + 1, st.g0) not in SPARE:
                    dve.wait_ge(diff_done[st.l + 1], st.g - 1)
                dve.tensor_tensor(state(st.l + 1, st)[:, :], n_sb[st.ring][:, :], zd[st.ring][:, :], ALU.add) \
                    .then_inc(h_done[st.l], 1)

            def final_candidate_input(st):
                dve.wait_ge(in_made[st.l], st.g + 1)
                dve.wait_ge(rh_done[st.l], st.g + 1)
                for cols in HALVES:
                    dve.tensor_tensor(rh[st.ring][:, cols], ps_in[:, cols], rh[st.ring][:, cols], ALU.add) \
                        .then_inc(pre_done[st.l], 1)

            def final_new_state(st):
                z, n, d = z_sb[st.ring], n_sb[st.ring], zd[st.ring]
                for k, cols in enumerate(HALVES):
                    dve.wait_ge(n_done[st.l], st.g + 1 + k)
                    dve.tensor_tensor(d[:, cols], state(st.l, st)[:, cols], n[:, cols], ALU.subtract) \
                        .then_inc(diff_done[st.l], 1)
                for k, cols in enumerate(HALVES):
                    dve.wait_ge(diff_done[st.l], st.g + 1 + k)
                    dve.wait_ge(z_done[st.l], st.g + 1 + k)
                    dve.tensor_tensor(d[:, cols], z[:, cols], d[:, cols], ALU.mult).then_inc(zd_done[st.l], 1)
                for k, cols in enumerate(HALVES):
                    dve.wait_ge(zd_done[st.l], st.g + 1 + k)
                    dve.tensor_tensor(h[L][st.parity][:, cols], n[:, cols], d[:, cols], ALU.add) \
                        .then_inc(h_done[st.l], 1)

            def final_residual(st):
                for k, cols in enumerate(HALVES):
                    dve.wait_ge(out_transposed, st.g + 1 + k)
                    dve.tensor_tensor(final_rows[:, cols], OUT_BANKS[k][:, cols],
                                      x_all[:, st.g * COLS + cols.start:st.g * COLS + cols.stop], ALU.add) \
                        .then_inc(out_ready, 1)

            def residual(st):
                dve.wait_ge(out_transposed, st.g + 1)
                if st.g0 >= 2 or st.in_loop:
                    dve.wait_ge(stored[st.parity], 16 * st.pair)
                dve.tensor_tensor(out_rows[st.parity][:, :, :].rearrange("n b d -> n (b d)"), ps_out[:, :],
                                  x_all[:, bass.ts(st.g, COLS)], ALU.add).then_inc(out_ready, 1)

            row_statistics(EARLY[0])
            aggregate_statistics(EARLY[0])
            centre(EARLY[0])
            mask(EARLY[0])
            scale(EARLY[0])
            dve.wait_ge(weights_hi, 1)
            dve.tensor_tensor(whh_lo[:, :], ps_whhT[:, 0:3 * P], whh_hi[:, :].bitcast(f32), ALU.subtract) \
                .then_inc(weights_lo, 1)
            row_statistics(EARLY[1])

            def v_part_lo(l):
                dve.wait_ge(weights_hi, l + 2)
                dve.tensor_tensor(v_lo[l][:, :], ps_v[l][:, 0:3 * P], v_hi[l][:, :].bitcast(f32), ALU.subtract) \
                    .then_inc(weights_lo, 1)

            def slot(s, it):
                def first_states_lo(when):
                    for st in prepared(s, it, "transpose", when):
                        if st.l == 0:
                            first_state_lo(st)

                first_states_lo("own")
                if s == 0:
                    aggregate_statistics(EARLY[1])
                    negate_mean(EARLY[1])
                for st in prepared(s, it, "aggregate", "own"):
                    aggregate_lo(st)
                if s == 0:
                    v_part_lo(0)
                    dve.wait_ge(b_loaded, 32)
                    dve.tensor_tensor(b_rz[:, :], bi[:, 0:2], bh[:, 0:2], ALU.add).then_inc(bias_ready, 1)
                    scale(EARLY[1])
                    row_statistics(EARLY[2])
                for st in first_steps(s, it, 4, 3):
                    row_statistics(st)
                    mask(st)
                    aggregate_statistics(st)
                for st in first_steps(s, it, 3, 3):
                    centre(st)
                    scale(st)
                for st in gates(s, it):
                    reset_product(st)
                first_states_lo("early")
                if s == 0:
                    aggregate_statistics(EARLY[2])
                    negate_mean(EARLY[2])
                hurry = [st for st in gates(s - 1, it) if soon(st)]
                if hurry:
                    candidate_input(Step(s, it))
                    new_state(hurry[0])
                for st in prepared(s, it, "aggregate", "late"):
                    aggregate_lo(st)
                if not hurry:
                    for st in gates(s, it):
                        if st.n == FINAL.n:
                            final_candidate_input(st)
                        else:
                            candidate_input(st)
                if s == 0:
                    scale(EARLY[2])
                first_states_lo("late")
                for st in gates(s - 1, it):
                    if st.n == FINAL.n:
                        final_new_state(st)
                    elif not soon(st):
                        new_state(st)
                for st in gates(s - 2, it):
                    if st.n == FINAL.n:
                        final_residual(st)
                    elif st.l == L - 1 and s < FINAL.n:
                        residual(st)
                if s in V_TAKEN:
                    v_part_lo(V_TAKEN[s])

            run_slots(dve, slot)

        @block.tensor
        def _(pe):
            def transpose4(dst, src):
                for b in range(PER):
                    ins = pe.transpose(dst[:, b * P:(b + 1) * P], src[:, b * P:(b + 1) * P], ident[:, :])
                return ins

            def transpose_state(st):
                if st.l == 0:
                    src = relu_nat[st.parity]
                    pe.wait_ge(relu_done, st.g + 1)
                else:
                    src = state(st.l, st)
                    pe.wait_ge(h_done[st.l - 1], st.g + 1)
                last = transposed_before(st)
                if last and last.l == 0:
                    pe.wait_ge(h_lo_done[0], last.g + 1)
                elif last:
                    pe.wait_ge(nat_done[last.l], last.g + 1)
                transpose4(ps_t[st.n % 2], src).then_inc(transposed[st.l], 1)

            def transpose_out(st):
                pe.wait_ge(h_done[L - 1], st.g + 1)
                if st.n == FINAL.n - 1:
                    pe.wait_ge(rows_copied, 1)
                elif st.g0 or st.in_loop:
                    pe.wait_ge(out_ready, st.g)
                transpose4(ps_out, h[L][st.parity]).then_inc(out_transposed, 1)

            def final_transpose_out(st):
                for k, cols in enumerate(HALVES):
                    pe.wait_ge(h_done[L - 1], st.g + 1 + k)
                    for b in range(cols.start, cols.stop, P):
                        ins = pe.transpose(OUT_BANKS[k][:, b:b + P], h[L][st.parity][:, b:b + P], ident[:, :])
                    ins.then_inc(out_transposed, 1)

            def aggregate(st):
                if st.l == 0:
                    rows = relu_nat[st.parity]
                    pe.wait_ge(relu_done, st.g + 1)
                    wait_for_mask(pe, st.g)
                else:
                    rows = nat[st.ring]
                    pe.wait_ge(nat_done[st.l], st.g + 1)
                last = st.before()
                if last:
                    pe.wait_ge(g_lo_done[last.l], last.g + 1)
                for b in range(PER):
                    cols = slice(b * P, (b + 1) * P)
                    ins = pe.matmul(ps_g[:, cols], rows[:, cols], mask_all[:, bass.ds(st.g * COLS + b * N, N)],
                                    start=True, stop=True)
                ins.then_inc(aggregated[st.l], 1)

            def product(ps, w_hi, w_lo, gate, a_hi, a_lo, start, stop, cols=slice(0, COLS)):
                rows = slice(gate * P, (gate + 1) * P)
                pe.matmul(ps[:, cols], w_hi[:, rows], a_hi[:, cols], start=start, stop=False)
                pe.matmul(ps[:, cols], w_hi[:, rows], a_lo[:, cols], start=False, stop=False)
                return pe.matmul(ps[:, cols], w_lo[:, rows], a_hi[:, cols], start=False, stop=stop)

            def state_part(st, ps, gate, stop, **part):
                return product(ps, whh_hi, whh_lo, gate, h_hi[st.l][st.parity], h_lo[st.l][st.parity], True, stop, **part)

            def aggregate_part(st, ps, gate, start, **part):
                return product(ps, v_hi[st.l], v_lo[st.l], gate, g_hi[st.ring], g_lo[st.ring], start, True, **part)

            def hidden_candidate(st):
                pe.wait_ge(h_hi_done[st.l], st.g + 1)
                pe.wait_ge(h_lo_done[st.l], st.g + 1)
                last = st.before()
                if last:
                    pe.wait_ge(rh_done[last.l], last.g + 1)
                state_part(st, ps_hn, 2, True).then_inc(hn_made[st.l], 1)

            def reset(st):
                pe.wait_ge(h_hi_done[st.l], st.g + 1)
                pe.wait_ge(h_lo_done[st.l], st.g + 1)
                last = st.before()
                if last:
                    pe.wait_ge(r_done[last.l], last.g + 1)
                state_part(st, ps_r, 0, False)
                pe.wait_ge(g_hi_done[st.l], st.g + 1)
                pe.wait_ge(g_lo_done[st.l], st.g + 1)
                if st.g0 == 0 and not st.in_loop:
                    pe.wait_ge(weights_lo, st.l + 2)
                aggregate_part(st, ps_r, 0, False).then_inc(r_made[st.l], 1)

            def input_candidate(st):
                last = st.before()
                if last:
                    pe.wait_ge(pre_done[last.l], last.g + 1)
                aggregate_part(st, ps_in, 2, True).then_inc(in_made[st.l], 1)

            def update(st):
                last = st.before()
                if last:
                    pe.wait_ge(z_done[last.l], last.g + 1)
                for ps, cols in zip(Z_BANKS, HALVES) if st.n == FINAL.n else [(ps_z, slice(0, COLS))]:
                    state_part(st, ps, 1, False, cols=cols)
                    aggregate_part(st, ps, 1, False, cols=cols).then_inc(z_made[st.l], 1)

            def keep_busy(n):
                for _ in range(n):
                    pe.matmul(ps_g[:, 0:P], ident[:, :], ident[:, :], start=True, stop=True)

            pe.wait_ge(ident_ready, 1)
            keep_busy(8)
            pe.wait_ge(whh_loaded, 16)
            for c in range(3):
                ins = pe.transpose(ps_whhT[:, c * P:(c + 1) * P], whh_nat[:, c, :], ident[:, :])
            ins.then_inc(whhT_made, 1)
            pe.wait_ge(w_loaded, 16)
            for l in range(L):
                ins = pe.transpose(ps_wT[:, l * P:(l + 1) * P], w_nat[:, l, :], ident[:, :])
            ins.then_inc(wT_made, 1)
            pe.wait_ge(wih_loaded, 16)
            for c in range(3):
                ins = pe.transpose(ps_wihT[:, c * P:(c + 1) * P], wih_nat[:, c, :], ident[:, :])
            ins.then_inc(wihT_made, 1)

            def make_v(l):
                if l == 0:
                    pe.wait_ge(wT_ready, 1)
                    pe.wait_ge(wihT_ready, 1)
                if l == 2:
                    pe.wait_ge(weights_lo, 3)
                pe.matmul(ps_v[l][:, 0:3 * P], wT[:, l, :], wihT[:, :], start=True, stop=True).then_inc(v_made, 1)

            def slot(s, it):
                def transposes(when):
                    for st in prepared(s, it, "transpose", when):
                        transpose_state(st)

                def aggregates(when):
                    for st in prepared(s, it, "aggregate", when):
                        aggregate(st)

                transposes("own")
                if s == 0:
                    aggregates("own")
                    make_v(0)
                    pe.wait_ge(weights_lo, 1)
                if s != FINAL.n:
                    for st in gates(s, it):
                        hidden_candidate(st)
                if s:
                    aggregates("own")
                    transposes("early")
                for st in gates(s, it):
                    reset(st)
                if s == FINAL.n:
                    hidden_candidate(FINAL)
                    transpose_out(Step(s - 2, it))
                if s == 0:
                    input_candidate(EARLY[0])
                    transposes("early")
                aggregates("late")
                transposes("late")
                for st in gates(s - 2, it):
                    if st.n == FINAL.n:
                        final_transpose_out(st)
                    elif st.l == L - 1 and s != FINAL.n:
                        transpose_out(st)
                for st in gates(s, it):
                    if s:
                        input_candidate(st)
                    update(st)
                if s in V_MADE:
                    make_v(V_MADE[s])

            run_slots(pe, slot)


_INS = ["x", "adj", "L0_gnn_weight", "L0_gnn_w_ih", "L0_gnn_w_hh", "L0_gnn_b_ih", "L0_gnn_b_hh"]
_OUTS = [((64, 128, 128), "float32")]


def kernel(**inputs):
    import numpy as _np
    import concourse.bacc as _bacc
    from concourse import mybir as _mybir
    from concourse.bass_utils import run_bass_kernel_spmd as _run

    nc = _bacc.Bacc("TRN2", target_bir_lowering=False, num_devices=1)
    arrays, args = {}, []
    for name in _INS:
        a = _np.ascontiguousarray(inputs[name])
        arrays[f"in_{name}_dram"] = a
        args.append(nc.dram_tensor(f"in_{name}_dram", a.shape, _mybir.dt.from_np(a.dtype), kind="ExternalInput").ap())
    for i, (shape, dtype) in enumerate(_OUTS):
        dt = _mybir.dt.from_np(_np.dtype(dtype))
        args.append(nc.dram_tensor(f"out_{i}_dram", shape, dt, kind="ExternalOutput").ap())
    gnn_residual_kernel(nc, *args)
    r = _run(nc, [arrays], core_ids=[0])
    return r.results[0]["out_0_dram"]
```
